# Optimizing a Trainium2 kernel written in Bass

```python
import numpy as np
import jax
import jax.numpy as jnp

def _softmax(x, axis=-1):
    return jax.nn.softmax(x, axis=axis)

def _gelu(x):
    return jax.nn.gelu(x, approximate=True)

def _silu(x):
    return jax.nn.silu(x)

def _sigmoid(x):
    return jax.nn.sigmoid(x)

def _layernorm(x, axis=-1, eps=1e-05):
    m = jnp.mean(x, axis=axis, keepdims=True)
    v = jnp.var(x, axis=axis, keepdims=True)
    return (x - m) / jnp.sqrt(v + eps)

def _scatter_add(tgt, idx, src, axis=0):
    return tgt.at[idx].add(src)

def _segment_sum(src, seg, n):
    return jax.ops.segment_sum(src, seg, n)
kernel_name = 'mk_xattn_ffn_d1_seqx_r4_7411a9'

def setup_inputs(seed: int=0):
    np.random.seed(seed)
    _w = jnp.asarray

    def _rec_inputs():
        import jax
        import jax.numpy as jnp
        _rk = jax.random.key(seed)
        x = -0.0005207 + 1.001 * jax.random.normal(jax.random.fold_in(_rk, 1), (2, 512, 256), jnp.float32)
        _lenS = 512 - jax.random.randint(jax.random.fold_in(_rk, 7), (2,), 0, max(1, 512 // 4) + 1, jnp.int32)
        _lenS2 = 1024 - jax.random.randint(jax.random.fold_in(_rk, 8), (2,), 0, max(1, 1024 // 4) + 1, jnp.int32)
        _ctx_1024P = jax.random.normal(jax.random.fold_in(_rk, 11), (2, 16, 256), jnp.float32)
        _ctx_1024c = jax.random.dirichlet(jax.random.fold_in(_rk, 511), 0.3 * jnp.ones((16,), jnp.float32), (2, 1024))
        _ctx_1024t = jnp.einsum('bsk,bkd->bsd', _ctx_1024c, _ctx_1024P)
        _ctx_1024t = _ctx_1024t * jax.lax.rsqrt(jnp.mean(jnp.square(_ctx_1024t)) + 1e-12) * 0.953939
        ctx_1024 = -1.52775e-05 + 0.999936 * (_ctx_1024t + 0.3 * jax.random.normal(jax.random.fold_in(_rk, 611), (2, 1024, 256), jnp.float32))
        return (x, ctx_1024)
    x, ctx_1024 = _rec_inputs()

    def _L0_xattn_setup():
        import jax, jax.numpy as jnp
        import numpy as np
        DIM = 256
        HEADS = 16
        DHEAD = 64
        INNER = HEADS * DHEAD
        EPS = 1e-05

        def layer_norm(x, g, b):
            mu = jnp.mean(x, axis=-1, keepdims=True)
            var = jnp.mean(jnp.square(x - mu), axis=-1, keepdims=True)
            return (x - mu) * jax.lax.rsqrt(var + EPS) * g + b

        def apply_rope(x, cos, sin):
            d2 = x.shape[-1] // 2
            x1, x2 = (x[..., :d2], x[..., d2:])
            return jnp.concatenate([x1 * cos - x2 * sin, x2 * cos + x1 * sin], axis=-1)
        key = jax.random.key(seed)
        ks = jax.random.split(key, 10)
        B, N, S = (8, 64, 1024)
        latents = jax.random.normal(ks[0], (B, N, DIM), dtype=jnp.float32)
        context = jax.random.normal(ks[1], (B, S, DIM), dtype=jnp.float32)
        cos = jax.random.uniform(ks[2], (S, DHEAD // 2), dtype=jnp.float32)
        sin = jax.random.uniform(ks[3], (S, DHEAD // 2), dtype=jnp.float32)
        init = lambda k, shp, fan_in: jax.random.normal(k, shp, dtype=jnp.float32) / np.sqrt(fan_in)
        return {'latents': latents, 'context': context, 'cos': cos, 'sin': sin, 'ln_lat_g': jnp.ones((DIM,), jnp.float32), 'ln_lat_b': jnp.zeros((DIM,), jnp.float32), 'ln_ctx_g': jnp.ones((DIM,), jnp.float32), 'ln_ctx_b': jnp.zeros((DIM,), jnp.float32), 'Wq': init(ks[4], (DIM, INNER), DIM), 'Wkv': init(ks[5], (DIM, 2 * INNER), DIM), 'Wo': init(ks[6], (INNER, DIM), INNER), 'bo': jnp.zeros((DIM,), jnp.float32)}
    _L0_xattn_all = _L0_xattn_setup()
    _L0_xattn_in = {k: v for k, v in _L0_xattn_all.items() if k in ('cos', 'sin', 'ln_lat_g', 'ln_lat_b', 'ln_ctx_g', 'ln_ctx_b', 'Wq', 'Wkv', 'Wo', 'bo')}
    del _L0_xattn_all

    def _L0_ffn_setup():
        import jax, jax.numpy as jnp
        import numpy as np
        H = 256
        E = 8
        B, S = (4, 512)
        key = jax.random.key(seed)
        k1, k2, k3, k4 = jax.random.split(key, 4)
        x = jax.random.normal(k1, (B, S, H), dtype=jnp.float32)
        wg = jax.random.normal(k2, (H, E), dtype=jnp.float32) * 0.02
        W = jax.random.normal(k3, (E, H, H), dtype=jnp.float32) * 0.02
        b = jax.random.normal(k4, (E, H), dtype=jnp.float32) * 0.02
        return {'x': x, 'wg': wg, 'W': W, 'b': b}
    _L0_ffn_all = _L0_ffn_setup()
    _L0_ffn_in = {k: v for k, v in _L0_ffn_all.items() if k in ('wg', 'W', 'b')}
    del _L0_ffn_all
    return {'x': x, 'ctx_1024': ctx_1024, 'L0_xattn_cos': _L0_xattn_in['cos'], 'L0_xattn_sin': _L0_xattn_in['sin'], 'L0_xattn_ln_lat_g': _L0_xattn_in['ln_lat_g'], 'L0_xattn_ln_lat_b': _L0_xattn_in['ln_lat_b'], 'L0_xattn_ln_ctx_g': _L0_xattn_in['ln_ctx_g'], 'L0_xattn_ln_ctx_b': _L0_xattn_in['ln_ctx_b'], 'L0_xattn_Wq': _L0_xattn_in['Wq'], 'L0_xattn_Wkv': _L0_xattn_in['Wkv'], 'L0_xattn_Wo': _L0_xattn_in['Wo'], 'L0_xattn_bo': _L0_xattn_in['bo'], 'L0_ffn_wg': _L0_ffn_in['wg'], 'L0_ffn_W': _L0_ffn_in['W'], 'L0_ffn_b': _L0_ffn_in['b']}

def reference(x, ctx_1024, L0_xattn_cos, L0_xattn_sin, L0_xattn_ln_lat_g, L0_xattn_ln_lat_b, L0_xattn_ln_ctx_g, L0_xattn_ln_ctx_b, L0_xattn_Wq, L0_xattn_Wkv, L0_xattn_Wo, L0_xattn_bo, L0_ffn_wg, L0_ffn_W, L0_ffn_b):
    import jax
    import jax.numpy as jnp

    def _L0_xattn_ref(latents, context, cos, sin, ln_lat_g, ln_lat_b, ln_ctx_g, ln_ctx_b, Wq, Wkv, Wo, bo):
        import jax, jax.numpy as jnp
        import numpy as np
        DIM = 256
        HEADS = 16
        DHEAD = 64
        INNER = HEADS * DHEAD
        EPS = 1e-05

        def layer_norm(x, g, b):
            mu = jnp.mean(x, axis=-1, keepdims=True)
            var = jnp.mean(jnp.square(x - mu), axis=-1, keepdims=True)
            return (x - mu) * jax.lax.rsqrt(var + EPS) * g + b

        def apply_rope(x, cos, sin):
            d2 = x.shape[-1] // 2
            x1, x2 = (x[..., :d2], x[..., d2:])
            return jnp.concatenate([x1 * cos - x2 * sin, x2 * cos + x1 * sin], axis=-1)
        b, n, _ = latents.shape
        s = context.shape[1]
        lat = layer_norm(latents, ln_lat_g, ln_lat_b)
        ctx = layer_norm(context, ln_ctx_g, ln_ctx_b)
        q = (lat @ Wq).reshape(b, n, HEADS, DHEAD).transpose(0, 2, 1, 3)
        kv = ctx @ Wkv
        k, v = jnp.split(kv, 2, axis=-1)
        k = k.reshape(b, s, HEADS, DHEAD).transpose(0, 2, 1, 3)
        v = v.reshape(b, s, HEADS, DHEAD).transpose(0, 2, 1, 3)
        k = apply_rope(k, cos[None, None], sin[None, None])
        scale = DHEAD ** (-0.5)
        attn = jnp.einsum('bhnd,bhsd->bhns', q, k) * scale
        attn = jnp.clip(attn, -11.0, 11.0)
        attn = jax.nn.softmax(attn, axis=-1)
        out = jnp.einsum('bhns,bhsd->bhnd', attn, v)
        out = out.transpose(0, 2, 1, 3).reshape(b, n, INNER)
        return out @ Wo + bo

    def _L0_ffn_ref(x, wg, W, b):
        import jax, jax.numpy as jnp
        import numpy as np
        H = 256
        E = 8
        B, S = (4, 512)
        Bb, Ss, Hh = x.shape
        Ee = wg.shape[1]
        T = Bb * Ss
        C = T // Ee
        xt = x.reshape(T, Hh)
        logits = xt @ wg
        probs = jax.nn.softmax(logits, axis=-1)
        idx = jnp.argmax(probs, axis=-1)
        mask = jax.nn.one_hot(idx, Ee, dtype=xt.dtype)
        locations = jnp.cumsum(mask, axis=0) - mask
        mask = mask * (locations < C).astype(xt.dtype)
        gate = jnp.sum(probs * mask, axis=-1)
        loc_s = jnp.sum(locations * mask, axis=-1).astype(jnp.int32)
        loc_oh = jax.nn.one_hot(loc_s, C, dtype=xt.dtype)
        dispatch = mask[:, :, None] * loc_oh[:, None, :]
        combine = gate[:, None, None] * dispatch
        exp_in = jnp.einsum('tec,th->ech', dispatch, xt)
        exp_out = jnp.einsum('ech,efh->ecf', exp_in, W) + b[:, None, :]
        out = jnp.einsum('tec,ecf->tf', combine, exp_out)
        return out.reshape(Bb, Ss, Hh)
    x = x + _L0_xattn_ref(_layernorm(x, axis=-1), ctx_1024, L0_xattn_cos, L0_xattn_sin, L0_xattn_ln_lat_g, L0_xattn_ln_lat_b, L0_xattn_ln_ctx_g, L0_xattn_ln_ctx_b, L0_xattn_Wq, L0_xattn_Wkv, L0_xattn_Wo, L0_xattn_bo)
    x = x + _L0_ffn_ref(_layernorm(x, axis=-1), L0_ffn_wg, L0_ffn_W, L0_ffn_b)
    return x

_drawn_inputs = setup_inputs


def setup_inputs(seed=0):
    import zlib

    import numpy as np

    out = dict(_drawn_inputs(seed))
    spreads = {'L0_xattn_ln_lat_g': (1.0, 0.6),
     'L0_xattn_ln_lat_b': (0.0, 0.592),
     'L0_xattn_ln_ctx_g': (1.0, 0.2),
     'L0_xattn_ln_ctx_b': (0.0, 0.1),
     'L0_xattn_bo': (0.0, 0.1)}
    factors = {'L0_xattn_cos': 5.051, 'L0_xattn_sin': 5.285, 'L0_ffn_b': 21.341}
    for name, (base, spread) in spreads.items():
        noise = np.random.default_rng([zlib.crc32(name.encode()), seed]).standard_normal(out[name].shape)
        drawn = base * np.exp(spread * noise) if base else spread * noise
        out[name] = jnp.asarray(drawn.astype(out[name].dtype))
    for name, factor in factors.items():
        out[name] = (out[name] * factor).astype(out[name].dtype)
    return out
```

```python
import concourse.bass as bass
from concourse import mybir
from concourse.alu_op_type import AluOpType as ALU
from contextlib import ExitStack
import math

FP32 = mybir.dt.float32
FP32R = mybir.dt.float32r
BF16 = mybir.dt.bfloat16
ACT = mybir.ActivationFunctionType
AX = mybir.AxisListType

PART = 128
BANK = 512
HEADS, DHEAD = 16, 64
EPS = 1e-5
CLIP = 11.0
SCALE = DHEAD ** -0.5
E_MIN, E_MAX = math.exp(-CLIP), math.exp(CLIP)


def xattn_moe_kernel(nc, x, ctx_1024, cos, sin, lat_g, lat_b, ctx_g, ctx_b, Wq, Wkv, Wo, bo, wg, W, b, out):
    BATCH, N, DIM = x.shape
    S = ctx_1024.shape[1]
    E = wg.shape[1]
    INNER = HEADS * DHEAD
    KT = DIM // PART
    NT = BATCH * N // PART
    NTB = N // PART
    ST = S // PART
    STA = BATCH * ST
    PAIRS = HEADS // 2
    PW = 2 * DHEAD
    PIECES = ST // 2
    CAP = BATCH * N // E
    assert BATCH == 2 and N == BANK and PW == PART and DIM == 256 and ST == 8

    x_v = x.rearrange("b (t p) d -> p (b t) d", p=PART)
    out_v = out.rearrange("b (t p) d -> p (b t) d", p=PART)
    ctx_v = ctx_1024.rearrange("b (t p) d -> p (b t) d", p=PART)
    cos_v = cos.rearrange("(t p) f -> p t f", p=PART)
    sin_v = sin.rearrange("(t p) f -> p t f", p=PART)
    Wq_v = Wq.rearrange("(k p) n -> p k n", p=PART)
    Wkv_v = Wkv.rearrange("(k p) (c n) -> p k c n", p=PART, c=2)
    Wo_v = Wo.rearrange("(r p) n -> p r n", p=PART)
    wg_v = wg.rearrange("(k p) e -> p k e", p=PART)
    W_v = W.rearrange("e (t p) h -> p (e t) h", p=PART)

    es = ExitStack()
    with es:
        def sb(name, shape, dt=FP32):
            return es.enter_context(nc.sbuf_tensor(name, shape, dt))

        def over(name, shape, place):
            return nc.alloc_sbuf_tensor_at(name, shape, FP32, offset=place)

        def sem(name):
            return es.enter_context(nc.semaphore(name))

        x_sb = sb("x_sb", [PART, NT, DIM])
        ctx_space = -(-nc.sbuf_base // 32) * 32
        ctxT_h = sb("ctxT_h", [PART, KT, STA * PART], FP32R)
        ctxT_l = sb("ctxT_l", [PART, KT, STA * PART], FP32R)
        x_space = -(-nc.sbuf_base // 32) * 32
        xT_h = sb("xT_h", [PART, KT, BATCH * N], FP32R)
        xT_l = sb("xT_l", [PART, KT, BATCH * N], FP32R)
        k_space = -(-nc.sbuf_base // 32) * 32
        k_stack = sb("k_stack", [PART, BATCH, 2, S], FP32R)
        q_high = sb("q_high", [PART, BATCH, 2, N], FP32R)
        q_low = sb("q_low", [PART, BATCH, 2, N], FP32R)
        v_sb = sb("v_sb", [PART, BATCH, ST, PW])
        P_SLOTS = 4
        probs = sb("probs", [PART, P_SLOTS, 2, N])
        psum_acc = sb("psum_acc", [PART, BATCH, 2 * N])
        cosT = sb("cosT", [PART, ST, 2, 2, DHEAD // 2])
        sinT = sb("sinT", [PART, ST, 2, 2, DHEAD // 2])
        w_raw = sb("w_raw", [PART, KT, 3, PW])
        wkv_h = sb("wkv_h", [PART, KT, 2, PW], FP32R)
        wkv_l = sb("wkv_l", [PART, KT, 2, PW], FP32R)
        wq_h = sb("wq_h", [PART, KT, 2, 2, DHEAD], FP32R)
        wq_l = sb("wq_l", [PART, KT, 2, 2, DHEAD], FP32R)
        rope_a = sb("rope_a", [PART, 2, 2 * PW])
        rope_b = sb("rope_b", [PART, 2, 2 * PW])
        k_rot = sb("k_rot", [PART, 2, 2 * PW])
        k_nat = sb("k_nat", [PART, 2, 4, 2, DHEAD], FP32R)
        o_raw = sb("o_raw", [PART, BATCH, N])
        den_sb = sb("den_sb", [64, BATCH, N])
        den_t = sb("den_t", [PART, BATCH, 8])
        rden_t = sb("rden_t", [PART, BATCH, 8])
        rden_b = sb("rden_b", [PART, BATCH, N])
        attn_T = sb("attn_T", [PART, PAIRS, BATCH * N])
        wo_sb = sb("wo_sb", [PART, PAIRS, DIM])
        ident = sb("ident", [PART, PART])
        ones = sb("ones", [PART, 32])
        lng = sb("lng", [PART, 4, KT])
        bo_b = sb("bo_b", [PART, DIM])
        wg_sb = sb("wg_sb", [PART, KT, E])
        b_sb = sb("b_sb", [E, DIM])
        GR = STA + NT
        bn = sb("bn", [PART, GR, 6])
        mv = sb("mv", [PART, GR, 2])
        var = sb("var", [PART, GR])
        std = sb("std", [PART, GR])
        rs_a = sb("rs_a", [PART, GR])
        rs_b = sb("rs_b", [PART, GR])
        rstd = sb("rstd", [PART, GR])
        ones_b = sb("ones_b", [PART, PART], BF16)
        upper_b = sb("upper_b", [PART, PART], BF16)
        rank_w = sb("rank_w", [PART, E])
        logit = sb("logit", [PART, NT, E])
        lmax = sb("lmax", [PART, NT])
        shifted = sb("shifted", [PART, NT, E])
        expd = sb("expd", [PART, NT, E])
        esum = sb("esum", [PART, NT])
        gate = sb("gate", [PART, NT])
        first = sb("first", [PART, NT, E])
        fmax = sb("fmax", [PART, NT])
        mask = sb("mask", [PART, NT, E])
        mask_b = sb("mask_b", [PART, NT, E], BF16)
        mask_sum = sb("mask_sum", [PART, NT, E], BF16)
        weight = sb("weight", [PART, NT, E])
        ctx_n = attn_T[:, 0:4, :].rearrange("p a (t d) -> p (a t) d", d=DIM)
        x_n = probs[:, :, :, :].rearrange("p a h (t d) -> p (a h t) d", d=DIM)[:, 0:NT, :]
        full = psum_acc[:, :, :].rearrange("p b (c n) -> p (b c) n", n=BANK)
        WT = over("WT", [PART, KT, E, DIM], ctx_space)
        W_nat = over("W_nat", [PART, E * KT, DIM], ctx_space + 4 * KT * E * DIM)
        weight_T = over("weight_T", [E, NT * PART], x_space)
        tile_bytes = 4 * NT * DIM
        x_1 = over("x_1", [PART, NT, DIM], k_space)
        x_1n = over("x_1n", [PART, NT, DIM], k_space + tile_bytes)
        x_1T = over("x_1T", [PART, KT, NT * PART], k_space + 2 * tile_bytes)
        acc = over("acc", [PART, NT, DIM], k_space + 3 * tile_bytes)

        psum = es.enter_context(nc.psum_tensor("psum", [PART, 8, BANK], FP32))
        scores = [psum[:, 0:2, :], psum[:, 2:4, :]]
        PROJ = (4, 5)
        o_ps = psum[:, 6, :]
        den_ps = psum[:, 7, :]
        scratch = nc.dram_tensor("rden_scratch", [BATCH, 2 * N], FP32, kind="Internal").ap()

        x_loaded, ctx_loaded, consts_loaded = sem("x_loaded"), sem("ctx_loaded"), sem("consts_loaded")
        cs_loaded, tail_loaded, consts_made = sem("cs_loaded"), sem("tail_loaded"), sem("consts_made")
        dve_step = sem("dve_step")
        pool_step = sem("pool_step")
        var_ready, std_ready = sem("var_ready"), sem("std_ready")
        ctx_normed, x_normed = sem("ctx_normed"), sem("x_normed")
        turned, turned_high, turned_low = sem("turned"), sem("turned_high"), sem("turned_low")
        w_turned, w_copied = sem("w_turned"), sem("w_copied")
        w_loaded, w_high, w_split = sem("w_loaded"), sem("w_high"), sem("w_split")
        kv_done, kt_done, q_done = sem("kv_done"), sem("kt_done"), sem("q_done")
        v_copied, kt_copied, q_copied, q_split = sem("v_copied"), sem("kt_copied"), sem("q_copied"), sem("q_split")
        rope_terms, rope_sums, k_ready = sem("rope_terms"), sem("rope_sums"), sem("k_ready")
        s_done, exp_done, clipped, summed = sem("s_done"), sem("exp_done"), sem("clipped"), sem("summed")
        av_done, o_copied, den_done, den_copied = sem("av_done"), sem("o_copied"), sem("den_done"), sem("den_copied")
        den_turned, rden_made, rden_stored = sem("den_turned"), sem("rden_made"), sem("rden_stored")
        rden_spread, heads_normed = sem("rden_spread"), sem("heads_normed")
        bias_added = sem("bias_added")
        wo_done, x1_made, x1n_made = sem("wo_done"), sem("x1_made"), sem("x1n_made")
        x1_turned, x1T_copied, logits_done, logits_used = sem("x1_turned"), sem("x1T_copied"), sem("logits_done"), sem("logits_used")
        shifted_made, expd_made, mask_made = sem("shifted_made"), sem("expd_made"), sem("mask_made")
        ranks_done, weight_made, weight_turned = sem("ranks_done"), sem("weight_made"), sem("weight_turned")
        weightT_copied, bias_done, bias_used = sem("weightT_copied"), sem("bias_done"), sem("bias_used")
        ffn_done, ffn_added, out_stored = sem("ffn_done"), sem("ffn_added"), sem("out_stored")

        UNITS = 2 * PAIRS
        last_unit = UNITS - 1
        TURNS = 4 * BATCH * KT // 2 + BATCH * KT
        CTX_TURNS = BATCH * KT * (ST // 4)

        def above_zero(value):
            return not isinstance(value, int) or value > 0

        def turn_group(g):
            if g < CTX_TURNS:
                t4, k = divmod(g, KT)
                cols = slice(4 * t4 * PART, (4 * t4 + 4) * PART)
                return ctx_n, 4 * t4, k, ctxT_h[:, k, cols], ctxT_l[:, k, cols], 2
            t4, k = divmod(g - CTX_TURNS, KT)
            cols = slice(4 * t4 * PART, (4 * t4 + 4) * PART)
            return x_n, 4 * t4, k, xT_h[:, k, cols], xT_l[:, k, cols], 0

        def kv_bank(p):
            return 0 if p == 0 else 1

        block = es.enter_context(nc.Block())

        @block.sync
        def _(sp):
            sp.dma_start(x_sb[:, :, :], x_v).then_inc(x_loaded, 16)
            for h in range(4):
                sp.dma_start(ctx_n[:, 4 * h:4 * h + 4, :], ctx_v[:, 4 * h:4 * h + 4, :]).then_inc(ctx_loaded, 16)

            def count(value):
                return value if isinstance(value, int) else sp.snap(sp.to_reg(value))

            sp.dma_start(w_raw[:, :, 0, :], Wq_v[:, :, 0:PW]).then_inc(w_loaded, 16)
            for c in range(2):
                sp.dma_start(w_raw[:, :, 1 + c, :], Wkv_v[:, :, c, 0:PW]).then_inc(w_loaded, 16)
            for h in range(2):
                sp.dma_start(cosT[:, :, h, 0, :], cos_v).then_inc(cs_loaded, 16)
                sp.dma_start(cosT[:, :, h, 1, :], cos_v).then_inc(cs_loaded, 16)
                sp.dma_start(sinT[:, :, h, 0, :], sin_v).then_inc(cs_loaded, 16)
                sp.dma_start(sinT[:, :, h, 1, :], sin_v).then_inc(cs_loaded, 16)
            sp.dma_start(wo_sb[:, :, :], Wo_v).then_inc(tail_loaded, 16)
            sp.dma_start(wg_sb[:, :, :], wg_v).then_inc(tail_loaded, 16)
            sp.dma_start(b_sb[:, :], b).then_inc(tail_loaded, 16)

            def sum_counts(u):
                return count(u - 1), count(u + 1), count(16 * (u + 1))

            def spread_sums(counts, b_):
                before, done, stored = counts
                sp.wait_ge(den_copied, done)
                for h in range(2):
                    sp.dma_start(den_t[64 * h:64 * h + 64, b_, :], den_sb[32 * h:32 * h + 1, b_, :]).then_inc(den_turned, 16)
                sp.wait_ge(rden_made, done)
                sp.dma_start(scratch[b_, :].rearrange("(p c) -> p c", c=8), rden_t[:, b_, :]).then_inc(rden_stored, 16)
                sp.wait_ge(rden_stored, stored)
                if above_zero(before):
                    sp.wait_ge(heads_normed, before)
                for h in range(2):
                    sp.dma_start(rden_b[64 * h:64 * h + 64, b_, :],
                                 scratch[b_:b_ + 1, h * N:(h + 1) * N].broadcast_to([64, N])).then_inc(rden_spread, 16)

            def iteration(i, first=False):
                if not first:
                    sums_1 = sum_counts(2 * i - 1)
                sums_0 = sum_counts(2 * i)
                if not first:
                    spread_sums(sums_1, 1)
                spread_sums(sums_0, 0)

            iteration(0, first=True)
            with sp.Fori(1, PAIRS - 1) as i:
                iteration(i)
            spread_sums(sum_counts(last_unit - 2), 1)
            sp.wait_ge(kv_done, PIECES * UNITS)
            sp.dma_start(W_nat[:, :, :], W_v).then_inc(tail_loaded, 16)
            spread_sums(sum_counts(last_unit - 1), 0)
            spread_sums(sum_counts(last_unit), 1)
            for g in range(BATCH):
                sp.wait_ge(ffn_added, (g + 1) * NTB * E)
                sp.dma_start(out_v[:, g * NTB:(g + 1) * NTB, :], acc[:, g * NTB:(g + 1) * NTB, :]).then_inc(out_stored, 16)
            sp.wait_ge(out_stored, 16 * BATCH)

        @block.gpsimd
        def _(pool):
            steps = [0]

            def then(ins):
                steps[0] += 1
                ins.then_inc(pool_step, 1)
                pool.wait_ge(pool_step, steps[0])

            then(nc.gpsimd.memset(ident[:, :], 0.0))
            nc.gpsimd.affine_select(out=ident[:, :], in_=ident[:, :], compare_op=ALU.not_equal, fill=1.0, base=0,
                                    pattern=[[-1, PART]], channel_multiplier=1).then_inc(consts_made, 1)
            nc.gpsimd.memset(ones[:, :], 1.0).then_inc(consts_made, 1)
            with nc.allow_non_contiguous_dma(reason="256 values each"):
                for n, v in enumerate((lat_g, lat_b, ctx_g, ctx_b)):
                    pool.dma_start(lng[:, n, :], v.rearrange("(k p) -> p k", p=PART)).then_inc(consts_loaded, 16)
            pool.dma_start(bo_b[:, :], bo.rearrange("(o n) -> o n", o=1).broadcast_to([PART, DIM])).then_inc(consts_loaded, 16)

            one = ones[:, 0:1].unsqueeze(2).unsqueeze(3)

            def split_pair(i):
                pool.wait_ge(w_loaded, 48 * (i + 1))
                if above_zero(4 * i):
                    pool.wait_ge(q_done, 4 * i)
                raw_q = w_raw[:, :, 0, :].rearrange("p k (h d) -> p k h d", h=2)
                nc.gpsimd.tensor_tensor(wkv_h[:, :, :, :], w_raw[:, :, 1:3, :], one.broadcast_to([PART, KT, 2, PW]),
                                        ALU.mult).then_inc(w_high, 1)
                for c in range(2):
                    nc.gpsimd.tensor_copy(wq_h[:, :, :, c, :], raw_q).then_inc(w_high, 1)
                pool.wait_ge(w_high, 3 * (i + 1))
                nc.gpsimd.tensor_tensor(wkv_l[:, :, :, :], w_raw[:, :, 1:3, :], wkv_h[:, :, :, :].bitcast(FP32),
                                        ALU.subtract).then_inc(w_split, 1)
                for c in range(2):
                    nc.gpsimd.tensor_tensor(wq_l[:, :, :, c, :], raw_q, wq_h[:, :, :, c, :].bitcast(FP32),
                                            ALU.subtract).then_inc(w_split, 1)

            pool.wait_ge(consts_made, 2)
            split_pair(0)
            nc.gpsimd.memset(ones_b[:, :], 1.0).then_inc(consts_made, 1)
            then(nc.gpsimd.memset(upper_b[:, :], 0.0))
            nc.gpsimd.affine_select(out=upper_b[:, :], in_=upper_b[:, :], compare_op=ALU.is_ge, fill=1.0, base=0,
                                    pattern=[[-1, PART]], channel_multiplier=1).then_inc(consts_made, 1)
            for e in range(E):
                last = nc.gpsimd.memset(rank_w[:, e:e + 1], float(E - e))
            last.then_inc(consts_made, 1)
            pool.wait_ge(x_normed, 2)
            pool.wait_ge(consts_loaded, 80)
            for t in range(NT):
                last = nc.gpsimd.tensor_tensor(x_sb[:, t, :], x_sb[:, t, :], bo_b[:, :], ALU.add)
            last.then_inc(bias_added, 1)
            split_pair(1)
            with pool.Fori(2, PAIRS) as i:
                split_pair(i)

        @block.scalar
        def _(act):
            act.wait_ge(var_ready, 1)
            nc.scalar.activation(std[:, :], var[:, :], ACT.Sqrt).then_inc(std_ready, 1)
            act.wait_ge(var_ready, 2)
            nc.scalar.activation(std[:, 0:NT], var[:, 0:NT], ACT.Sqrt).then_inc(std_ready, 1)
            act.wait_ge(consts_loaded, 80)
            for g in range(TURNS):
                _, _, k, high, _, c = turn_group(g)
                act.wait_ge(turned, g + 1)
                if g >= 4:
                    act.wait_ge(turned_low, g - 3)
                for dst in (full[:, g % 4, :], high):
                    nc.scalar.activation(dst, psum[:, g % 8, :], ACT.Identity, scale=lng[:, c, k:k + 1],
                                         bias=lng[:, c + 1, k:k + 1]).then_inc(turned_high, 1)

            def copy_w(g):
                ep, k = divmod(g, KT)
                act.wait_ge(w_turned, g + 1)
                nc.scalar.copy(WT[:, k, 2 * ep:2 * ep + 2, :],
                               psum[:, PROJ[g % 2], :].rearrange("p (e f) -> p e f", e=2)).then_inc(w_copied, 1)

            def copy_v(w, bw, p):
                act.wait_ge(kv_done, PIECES * w + p + 1)
                nc.scalar.copy(v_sb[:, bw, 2 * p:2 * p + 2, :],
                               psum[:, PROJ[kv_bank(p)], 2 * PW:4 * PW].rearrange("p (t n) -> p t n", t=2)).then_inc(v_copied, 1)

            def copy_kt(w, bw, p):
                act.wait_ge(kt_done, PIECES * w + p + 1)
                nc.scalar.copy(k_stack[:, bw, :, 2 * p * PART:(2 * p + 2) * PART],
                               psum[:, PROJ[0], :].rearrange("p (h s) -> p h s", h=2)).then_inc(kt_copied, 1)

            def copy_q(w, bw, h):
                act.wait_ge(q_done, 2 * w + h + 1)
                nc.scalar.copy(q_high[:, bw, h, :], psum[:, PROJ[1], :]).then_inc(q_copied, 1)

            def copy_o(u, b_):
                act.wait_ge(av_done, ST * (u + 1))
                if above_zero(u - 1):
                    act.wait_ge(heads_normed, u - 1)
                nc.scalar.copy(o_raw[:, b_, :], o_ps).then_inc(o_copied, 1)

            def copy_den(u, b_):
                act.wait_ge(den_done, u + 1)
                if above_zero(u - 1):
                    act.wait_ge(den_turned, 32 * (u - 1))
                nc.scalar.copy(den_sb[:, b_, :], den_ps[0:64, :]).then_inc(den_copied, 1)

            def load_pair(i):
                cols = bass.ds(i * PW, PW)
                act.wait_ge(w_split, 3 * i)
                act.dma_start(w_raw[:, :, 0, :], Wq_v[:, :, cols]).then_inc(w_loaded, 16)
                for c in range(2):
                    act.dma_start(w_raw[:, :, 1 + c, :], Wkv_v[:, :, c, cols]).then_inc(w_loaded, 16)

            def unit(u, b_, before=True, after=True, load=None):
                w, bw = u + 1, 1 - b_
                for j in range(ST):
                    if j == 1 and load is not None:
                        load_pair(load)
                    c = ST * u + j
                    act.wait_ge(s_done, c + 1)
                    if above_zero(c - P_SLOTS + 1):
                        act.wait_ge(av_done, c - P_SLOTS + 1)
                        jp = (j - P_SLOTS) % ST
                        act.wait_ge(summed, (ST - 1) * (u if j >= P_SLOTS else u - 1) + max(jp, 1))
                    nc.scalar.activation(probs[:, j % P_SLOTS, :, :], scores[j % 2], ACT.Exp, scale=SCALE).then_inc(exp_done, 1)
                    if before and j == 0:
                        copy_o(u - 1, bw)
                    if before and j == 1:
                        copy_den(u - 1, bw)
                    if after:
                        if j < PIECES:
                            copy_v(w, bw, j)
                        if 2 <= j < 2 + PIECES:
                            copy_kt(w, bw, j - 2)
                        if 4 <= j < 6:
                            copy_q(w, bw, j - 4)
                    else:
                        copy_w(j)

            for p in range(PIECES):
                copy_v(0, 0, p)
                copy_kt(0, 0, p)
            for h in range(2):
                copy_q(0, 0, h)
            unit(0, 0, before=False, load=1)
            unit(1, 1)
            with act.Fori(1, PAIRS - 1) as i:
                unit(2 * i, 0, load=i + 1)
                unit(2 * i + 1, 1)
            unit(last_unit - 1, 0)
            unit(last_unit, 1, after=False)
            copy_o(last_unit, 1)
            copy_den(last_unit, 1)

            for g in range(BATCH):
                ts = slice(g * NTB, (g + 1) * NTB)
                act.wait_ge(var_ready, 3 + g)
                nc.scalar.activation(std[:, ts], var[:, ts], ACT.Sqrt).then_inc(std_ready, 1)
                for k in range(KT):
                    act.wait_ge(x1_turned, KT * g + k + 1)
                    nc.scalar.copy(x_1T[:, k, g * N:(g + 1) * N], psum[:, 6 + k, :]).then_inc(x1T_copied, 1)
                act.wait_ge(shifted_made, g + 1)
                nc.scalar.activation(expd[:, ts, :], shifted[:, ts, :], ACT.Exp).then_inc(expd_made, 1)
                act.wait_ge(weight_turned, g + 1)
                nc.scalar.copy(weight_T[:, g * N:(g + 1) * N], psum[0:E, 4, :]).then_inc(weightT_copied, 1)

        @block.vector
        def _(dve):
            steps = [0]

            def then(ins):
                steps[0] += 1
                ins.then_inc(dve_step, 1)
                dve.wait_ge(dve_step, steps[0])

            def inverse_std(sl, ready):
                dve.wait_ge(std_ready, ready)
                then(nc.vector.reciprocal(rs_a[:, sl], std[:, sl]))
                then(nc.vector.tensor_tensor(rs_b[:, sl], rs_a[:, sl], rs_a[:, sl], ALU.mult))
                then(nc.vector.tensor_tensor(rs_b[:, sl], rs_b[:, sl], var[:, sl], ALU.mult))
                then(nc.vector.tensor_scalar(rs_b[:, sl], rs_b[:, sl], -0.5, 1.5, ALU.mult, ALU.add))
                then(nc.vector.tensor_tensor(rstd[:, sl], rs_a[:, sl], rs_b[:, sl], ALU.mult))

            def stats(tiles, at):
                for t in range(tiles.shape[1]):
                    last = nc.vector.bn_stats(bn[:, at + t, :], tiles[:, t, :])
                then(last)
                for t in range(tiles.shape[1]):
                    last = nc.vector.bn_aggr(mv[:, at + t, :], bn[:, at + t, :])
                then(last)

            def add_eps(sl):
                nc.vector.tensor_scalar(var[:, sl], mv[:, sl, 1], EPS, None, ALU.add).then_inc(var_ready, 1)

            def normalise(dst, src, t, at):
                return nc.vector.tensor_scalar(dst[:, t, :], src[:, t, :], mv[:, at + t, 0:1], rstd[:, at + t:at + t + 1],
                                               ALU.subtract, ALU.mult)

            dve.wait_ge(x_loaded, 16)
            stats(x_sb, 0)
            dve.wait_ge(ctx_loaded, 64)
            stats(ctx_n, NT)
            add_eps(slice(0, GR))
            inverse_std(slice(0, GR), 1)
            for t in range(NT):
                last = normalise(x_n, x_sb, t, 0)
            then(last)
            stats(x_n, 0)
            add_eps(slice(0, NT))
            for t in range(STA):
                normalise(ctx_n, ctx_n, t, NT).then_inc(ctx_normed, 1)
            inverse_std(slice(0, NT), 2)
            for t in range(NT):
                last = normalise(x_n, x_n, t, 0)
            last.then_inc(x_normed, 2)
            dve.wait_ge(cs_loaded, 128)
            then(nc.vector.tensor_scalar(sinT[:, :, :, 0, :], sinT[:, :, :, 0, :], -1.0, None, ALU.mult))
            for g in range(TURNS):
                _, _, _, high, low, _ = turn_group(g)
                dve.wait_ge(turned_high, 2 * (g + 1))
                nc.vector.tensor_tensor(low, full[:, g % 4, :], high.bitcast(FP32), ALU.subtract).then_inc(turned_low, 1)

            def rope(w, p):
                t = PIECES * w + p
                src = psum[:, PROJ[kv_bank(p)], 0:2 * PW].rearrange("p (a f c) -> p a f c", f=2, c=DHEAD // 2)
                cosv = cosT[:, 2 * p:2 * p + 2, :, :, :].rearrange("p t h f c -> p (t h) f c")
                sinv = sinT[:, 2 * p:2 * p + 2, :, :, :].rearrange("p t h f c -> p (t h) f c")
                a, bb, kr = rope_a[:, p % 2, :], rope_b[:, p % 2, :], k_rot[:, p % 2, :]
                a4 = a.rearrange("p (a f c) -> p a f c", f=2, c=DHEAD // 2)
                b4 = bb.rearrange("p (a f c) -> p a f c", f=2, c=DHEAD // 2)
                dve.wait_ge(v_copied, t + 1)
                nc.vector.tensor_tensor(a4, src, cosv, ALU.mult).then_inc(rope_terms, 1)
                nc.vector.tensor_tensor(b4, src[:, :, ::-1, :], sinv, ALU.mult).then_inc(rope_terms, 1)
                dve.wait_ge(rope_terms, 2 * (t + 1))
                if above_zero(t - 1):
                    dve.wait_ge(kt_done, t - 1)
                high = k_nat[:, p % 2, :, 0, :]
                nc.vector.tensor_tensor(high, a.rearrange("p (a d) -> p a d", a=4), bb.rearrange("p (a d) -> p a d", a=4),
                                        ALU.add).then_inc(rope_sums, 1)
                nc.vector.tensor_tensor(kr, a, bb, ALU.add).then_inc(rope_sums, 1)
                dve.wait_ge(rope_sums, 2 * (t + 1))
                nc.vector.tensor_tensor(k_nat[:, p % 2, :, 1, :], kr.rearrange("p (a d) -> p a d", a=4), high.bitcast(FP32),
                                        ALU.subtract).then_inc(k_ready, 1)

            def split_q(w, bw, h):
                dve.wait_ge(q_copied, 2 * w + h + 1)
                nc.vector.tensor_tensor(q_low[:, bw, h, :], psum[:, PROJ[1], :], q_high[:, bw, h, :].bitcast(FP32),
                                        ALU.subtract).then_inc(q_split, 1)

            def invert_sums(u, b_):
                dve.wait_ge(den_turned, 32 * (u + 1))
                if above_zero(u - 1):
                    dve.wait_ge(rden_stored, 16 * (u - 1))
                nc.vector.reciprocal(rden_t[:, b_, :], den_t[:, b_, :]).then_inc(rden_made, 1)

            def norm_heads(i, u, b_):
                dve.wait_ge(rden_spread, 32 * (u + 1))
                dve.wait_ge(o_copied, u + 1)
                dst = attn_T[:, bass.ds(i, 1), b_ * N:(b_ + 1) * N].rearrange("p o n -> p (o n)")
                nc.vector.tensor_tensor(dst, o_raw[:, b_, :], rden_b[:, b_, :], ALU.mult).then_inc(heads_normed, 1)

            def unit(i, u, b_, before=1, after=True):
                w, bw = u + 1, 1 - b_
                for j in range(ST):
                    c = ST * u + j
                    chunk = probs[:, j % P_SLOTS, :, :].rearrange("p h n -> p (h n)")
                    dve.wait_ge(exp_done, c + 1)
                    nc.vector.tensor_scalar(chunk, chunk, E_MIN, E_MAX, ALU.max, ALU.min).then_inc(clipped, 1)
                    if j >= 1:
                        dve.wait_ge(clipped, c + 1)
                        if j == 1 and before >= 2:
                            dve.wait_ge(den_done, u - 1)
                        if j >= 2:
                            dve.wait_ge(summed, (ST - 1) * u + j - 1)
                        prev = probs[:, 0, :, :].rearrange("p h n -> p (h n)") if j == 1 else psum_acc[:, b_, :]
                        nc.vector.tensor_tensor(psum_acc[:, b_, :], prev, chunk, ALU.add).then_inc(summed, 1)
                    if j == 1 and before >= 2:
                        norm_heads(i - 1, u - 2, b_)
                    if after and j < PIECES:
                        rope(w, j)
                    if j == 4 and before >= 1:
                        invert_sums(u - 1, bw)
                    if after and 4 <= j < 6:
                        split_q(w, bw, j - 4)

            for p in range(PIECES):
                rope(0, p)
            for h in range(2):
                split_q(0, 0, h)
            unit(0, 0, 0, before=0)
            unit(0, 1, 1, before=1)
            with dve.Fori(1, PAIRS - 1) as i:
                unit(i, 2 * i, 0, before=2)
                unit(i, 2 * i + 1, 1, before=2)
            unit(PAIRS - 1, last_unit - 1, 0, before=2)
            unit(PAIRS - 1, last_unit, 1, before=2, after=False)
            norm_heads(PAIRS - 1, last_unit - 1, 0)
            invert_sums(last_unit, 1)
            norm_heads(PAIRS - 1, last_unit, 1)

            for g in range(BATCH):
                tiles = range(g * NTB, (g + 1) * NTB)
                ts = slice(g * NTB, (g + 1) * NTB)
                dve.wait_ge(bias_added, 1)
                for n, t in enumerate(tiles):
                    dve.wait_ge(wo_done, t - n % 2 + 2)
                    last = nc.vector.tensor_tensor(x_1[:, t, :], psum[:, 4 + n // 2, (n % 2) * DIM:(n % 2 + 1) * DIM],
                                                   x_sb[:, t, :], ALU.add)
                    last.then_inc(x1_made, 1)
                dve.wait_ge(x1_made, (g + 1) * NTB)
                stats(x_1[:, ts, :], g * NTB)
                add_eps(ts)
                inverse_std(ts, 3 + g)
                for t in tiles:
                    normalise(x_1n, x_1, t, 0).then_inc(x1n_made, 1)
                dve.wait_ge(logits_done, g + 1)
                then(nc.vector.tensor_copy(logit[:, ts, :], psum[:, 4, 0:NTB * E].rearrange("p (t e) -> p t e", e=E)))
                then(nc.vector.reduce_max(lmax[:, ts], logit[:, ts, :], AX.X))
                nc.vector.tensor_tensor(shifted[:, ts, :], logit[:, ts, :], lmax[:, ts].unsqueeze(2).broadcast_to([PART, NTB, E]),
                                        ALU.subtract).then_inc(shifted_made, 1)
                dve.wait_ge(shifted_made, g + 1)
                then(nc.vector.scalar_tensor_tensor(out=first[:, ts, :], in0=shifted[:, ts, :], scalar=0.0,
                                                    in1=rank_w[:, :].unsqueeze(1).broadcast_to([PART, NTB, E]),
                                                    op0=ALU.is_equal, op1=ALU.mult))
                then(nc.vector.reduce_max(fmax[:, ts], first[:, ts, :], AX.X))
                then(nc.vector.tensor_tensor(mask[:, ts, :], first[:, ts, :], fmax[:, ts].unsqueeze(2).broadcast_to([PART, NTB, E]),
                                             ALU.is_equal))
                nc.vector.tensor_copy(mask_b[:, ts, :], mask[:, ts, :]).then_inc(mask_made, 1)
                dve.wait_ge(expd_made, g + 1)
                then(nc.vector.reduce_sum(esum[:, ts], expd[:, ts, :], AX.X))
                then(nc.vector.reciprocal(gate[:, ts], esum[:, ts]))
                dve.wait_ge(ranks_done, g + 1)
                then(nc.vector.scalar_tensor_tensor(out=weight[:, ts, :],
                                                    in0=psum[:, 5, 0:NTB * E].rearrange("p (t e) -> p t e", e=E),
                                                    scalar=float(CAP), in1=mask[:, ts, :], op0=ALU.is_lt, op1=ALU.mult))
                nc.vector.tensor_tensor(weight[:, ts, :], weight[:, ts, :], gate[:, ts].unsqueeze(2).broadcast_to([PART, NTB, E]),
                                        ALU.mult).then_inc(weight_made, 1)
                dve.wait_ge(weight_made, g + 1)
                for n, t in enumerate(tiles):
                    dve.wait_ge(bias_done, t - n % 2 + 2)
                    then(nc.vector.tensor_tensor(acc[:, t, :], psum[:, 6 + n // 2, (n % 2) * DIM:(n % 2 + 1) * DIM],
                                                 x_1[:, t, :], ALU.add))
                    for e in range(E):
                        dve.wait_ge(ffn_done, (t * E + e) // 2 + 1)
                        if e:
                            dve.wait_ge(ffn_added, t * E + e)
                        nc.vector.scalar_tensor_tensor(out=acc[:, t, :], in0=psum[:, e // 2, (e % 2) * DIM:(e % 2 + 1) * DIM],
                                                       scalar=weight[:, t, e:e + 1], in1=acc[:, t, :],
                                                       op0=ALU.mult, op1=ALU.add).then_inc(ffn_added, 1)

        @block.tensor
        def _(pe):
            pe.wait_ge(consts_made, 2)
            for g in range(TURNS):
                src, t0, k, _, _, _ = turn_group(g)
                if g >= 8:
                    pe.wait_ge(turned_high, 2 * (g - 7))
                if g < CTX_TURNS:
                    pe.wait_ge(ctx_normed, t0 + 4)
                else:
                    pe.wait_ge(x_normed, 2)
                for n in range(4):
                    last = nc.tensor.transpose(psum[:, g % 8, n * PART:(n + 1) * PART],
                                               src[:, t0 + n, k * PART:(k + 1) * PART], ident[:, :])
                last.then_inc(turned, 1)
            pe.wait_ge(turned_high, 2 * TURNS)
            pe.wait_ge(turned_low, TURNS)

            def project_kv(i, w, bw, p):
                if p == 0:
                    pe.wait_ge(w_split, 3 * (i + 1))
                    if above_zero(PIECES * w):
                        pe.wait_ge(kt_copied, PIECES * w)
                elif p == 1:
                    if above_zero(2 * w):
                        pe.wait_ge(q_split, 2 * w)
                else:
                    pe.wait_ge(rope_terms, 2 * (PIECES * w + p))
                bank = psum[:, PROJ[kv_bank(p)], :].rearrange("p (c t n) -> p c t n", c=2, t=2)
                for t in range(2):
                    cols = slice((bw * ST + 2 * p + t) * PART, (bw * ST + 2 * p + t + 1) * PART)
                    terms = [(a, w_) for k in range(KT) for a, w_ in
                             ((ctxT_h[:, k, cols], wkv_h[:, k, :, :]), (ctxT_h[:, k, cols], wkv_l[:, k, :, :]),
                              (ctxT_l[:, k, cols], wkv_h[:, k, :, :]))]
                    for n, (a, w_) in enumerate(terms):
                        last = nc.tensor.matmul(bank[:, :, t, :], a, w_, start=(n == 0), stop=(n == len(terms) - 1))
                last.then_inc(kv_done, 1)

            def turn_keys(w, p):
                pe.wait_ge(k_ready, PIECES * w + p + 1)
                if p > 0:
                    pe.wait_ge(kt_copied, PIECES * w + p)
                for h in range(2):
                    for t in range(2):
                        last = nc.tensor.transpose(psum[:, PROJ[0], (2 * h + t) * PART:(2 * h + t + 1) * PART],
                                                   k_nat[:, p % 2, 2 * t + h, :, :].rearrange("p a d -> p (a d)").bitcast(FP32),
                                                   ident[:, :])
                last.then_inc(kt_done, 1)

            def project_q(w, bw, h):
                if h == 0:
                    pe.wait_ge(rope_terms, 2 * PIECES * (w + 1))
                else:
                    pe.wait_ge(q_split, 2 * w + 1)
                cols = slice(bw * N, (bw + 1) * N)
                terms = [(w_, a) for k in range(KT) for w_, a in
                         ((wq_h[:, k, h], xT_h[:, k, cols]), (wq_h[:, k, h], xT_l[:, k, cols]),
                          (wq_l[:, k, h], xT_h[:, k, cols]))]
                for n, (w_, a) in enumerate(terms):
                    last = nc.tensor.matmul(psum[:, PROJ[1], :], w_.rearrange("p c d -> p (c d)"), a,
                                            start=(n == 0), stop=(n == len(terms) - 1))
                last.then_inc(q_done, 1)

            def score(u, b_, j):
                c = ST * u + j
                if j == 0:
                    pe.wait_ge(kt_copied, PIECES * (u + 1))
                    pe.wait_ge(q_split, 2 * (u + 1))
                if above_zero(c - 1):
                    pe.wait_ge(exp_done, c - 1)
                for h in range(2):
                    keys = k_stack[:, b_, h, j * PART:(j + 1) * PART]
                    nc.tensor.matmul(scores[j % 2][:, h, :], keys, q_high[:, b_, h, :], start=True, stop=False)
                    last = nc.tensor.matmul(scores[j % 2][:, h, :], keys, q_low[:, b_, h, :], start=False, stop=True)
                last.then_inc(s_done, 1)

            def weigh_values(u, b_, j):
                if j == 0:
                    pe.wait_ge(v_copied, PIECES * (u + 1))
                    if above_zero(u):
                        pe.wait_ge(o_copied, u)
                pe.wait_ge(clipped, ST * u + j + 1)
                for h in range(2):
                    last = nc.tensor.matmul(o_ps[64 * h:64 * h + 64, :], v_sb[:, b_, j, h * DHEAD:(h + 1) * DHEAD],
                                            probs[:, j % P_SLOTS, h, :], start=(j == 0), stop=(j == ST - 1))
                last.then_inc(av_done, 1)

            def sum_probs(u, b_):
                pe.wait_ge(summed, (ST - 1) * (u + 1))
                if above_zero(u):
                    pe.wait_ge(den_copied, u)
                for h in range(2):
                    last = nc.tensor.matmul(den_ps[32 * h:32 * h + 32, :], ones[:, :], psum_acc[:, b_, h * N:(h + 1) * N],
                                            start=True, stop=True)
                last.then_inc(den_done, 1)

            def turn_w(g):
                ep, k = divmod(g, KT)
                if g >= 2:
                    pe.wait_ge(w_copied, g - 1)
                for n in range(4):
                    last = nc.tensor.transpose(psum[:, PROJ[g % 2], n * PART:(n + 1) * PART],
                                               W_nat[:, 4 * ep + n, k * PART:(k + 1) * PART], ident[:, :])
                last.then_inc(w_turned, 1)

            def unit(i, u, b_, before=True, after=True):
                w, bw, iw = u + 1, 1 - b_, i + b_
                for j in range(ST):
                    if j < ST - 1:
                        score(u, b_, j + 1)
                    elif after:
                        score(w, bw, 0)
                    if before and j == 1:
                        sum_probs(u - 1, bw)
                    if after:
                        if 2 <= j < 2 + PIECES:
                            turn_keys(w, j - 2)
                        if j < PIECES:
                            project_kv(iw, w, bw, j)
                        if 4 <= j < 6:
                            project_q(w, bw, j - 4)
                    else:
                        if j == 0:
                            pe.wait_ge(tail_loaded, 64)
                        turn_w(j)
                    weigh_values(u, b_, j)

            project_kv(0, 0, 0, 0)
            project_kv(0, 0, 0, 1)
            for p in range(2, PIECES):
                turn_keys(0, p - 2)
                project_kv(0, 0, 0, p)
            for h in range(2):
                turn_keys(0, h + 2)
                project_q(0, 0, h)
            score(0, 0, 0)
            unit(0, 0, 0, before=False)
            unit(0, 1, 1)
            with pe.Fori(1, PAIRS - 1) as i:
                unit(i, 2 * i, 0)
                unit(i, 2 * i + 1, 1)
            unit(PAIRS - 1, last_unit - 1, 0)
            unit(PAIRS - 1, last_unit, 1, after=False)
            sum_probs(last_unit, 1)

            for g in range(BATCH):
                ts = slice(g * NTB, (g + 1) * NTB)
                tiles = range(g * NTB, (g + 1) * NTB)
                pe.wait_ge(heads_normed, last_unit + g)
                if g == 0:
                    pe.wait_ge(w_copied, E)
                else:
                    pe.wait_ge(weightT_copied, g)
                for n, t in enumerate(tiles):
                    for r in range(PAIRS):
                        last = nc.tensor.matmul(psum[:, 4 + n // 2, (n % 2) * DIM:(n % 2 + 1) * DIM],
                                                attn_T[:, r, t * PART:(t + 1) * PART], wo_sb[:, r, :],
                                                start=(r == 0), stop=(r == PAIRS - 1))
                    last.then_inc(wo_done, 1)
                pe.wait_ge(x1n_made, (g + 1) * NTB)
                if g:
                    pe.wait_ge(ffn_added, g * NTB * E)
                for k in range(KT):
                    for n, t in enumerate(tiles):
                        last = nc.tensor.transpose(psum[:, 6 + k, n * PART:(n + 1) * PART],
                                                   x_1n[:, t, k * PART:(k + 1) * PART], ident[:, :])
                    last.then_inc(x1_turned, 1)
                pe.wait_ge(x1T_copied, KT * (g + 1))
                for n, t in enumerate(tiles):
                    for k in range(KT):
                        last = nc.tensor.matmul(psum[:, 4, n * E:(n + 1) * E], x_1T[:, k, t * PART:(t + 1) * PART],
                                                wg_sb[:, k, :], start=(k == 0), stop=(k == KT - 1))
                last.then_inc(logits_done, 1)

                def experts(t):
                    for ep in range(E // 2):
                        if t > 0:
                            pe.wait_ge(ffn_added, (t - 1) * E + 2 * ep + 2)
                        for k in range(KT):
                            last = nc.tensor.matmul(psum[:, ep, :], x_1T[:, k, t * PART:(t + 1) * PART],
                                                    WT[:, k, 2 * ep:2 * ep + 2, :].rearrange("p e f -> p (e f)"),
                                                    start=(k == 0), stop=(k == KT - 1))
                        last.then_inc(ffn_done, 1)

                experts(tiles[0])
                pe.wait_ge(consts_made, 5)
                pe.wait_ge(mask_made, g + 1)
                for n, t in enumerate(tiles):
                    for t2 in range(t + 1):
                        last = nc.tensor.matmul(psum[:, 5, n * E:(n + 1) * E], (upper_b if t2 == t else ones_b)[:, :],
                                                mask_b[:, t2, :], start=(t2 == 0), stop=(t2 == t))
                last.then_inc(ranks_done, 1)
                pe.wait_ge(weight_made, g + 1)
                for n, t in enumerate(tiles):
                    last = nc.tensor.transpose(psum[0:E, 4, n * PART:(n + 1) * PART], weight[:, t, :], ident[:, :])
                last.then_inc(weight_turned, 1)
                pe.wait_ge(weightT_copied, g + 1)
                for n, t in enumerate(tiles):
                    nc.tensor.matmul(psum[:, 6 + n // 2, (n % 2) * DIM:(n % 2 + 1) * DIM],
                                     weight_T[:, t * PART:(t + 1) * PART], b_sb[:, :], start=True, stop=True).then_inc(bias_done, 1)
                for t in tiles[1:]:
                    experts(t)


_INS = ['x', 'ctx_1024', 'L0_xattn_cos', 'L0_xattn_sin', 'L0_xattn_ln_lat_g', 'L0_xattn_ln_lat_b', 'L0_xattn_ln_ctx_g',
        'L0_xattn_ln_ctx_b', 'L0_xattn_Wq', 'L0_xattn_Wkv', 'L0_xattn_Wo', 'L0_xattn_bo', 'L0_ffn_wg', 'L0_ffn_W', 'L0_ffn_b']
_OUTS = [((2, 512, 256), 'float32')]


def kernel(**inputs):
    import numpy as _np
    import concourse.bacc as _bacc
    from concourse import mybir as _mybir
    from concourse.bass_utils import run_bass_kernel_spmd as _run

    nc = _bacc.Bacc("TRN2", target_bir_lowering=False, num_devices=1)
    arrays, args = {}, []
    for name in _INS:
        a = _np.ascontiguousarray(inputs[name])
        arrays[f"in_{name}_dram"] = a
        args.append(nc.dram_tensor(f"in_{name}_dram", a.shape, _mybir.dt.from_np(a.dtype), kind="ExternalInput").ap())
    for i, (shape, dtype) in enumerate(_OUTS):
        dt = _mybir.dt.from_np(_np.dtype(dtype))
        args.append(nc.dram_tensor(f"out_{i}_dram", shape, dt, kind="ExternalOutput").ap())
    xattn_moe_kernel(nc, *args)
    r = _run(nc, [arrays], core_ids=[0])
    return r.results[0]["out_0_dram"]
```

```python
import concourse.bass as bass
from concourse import mybir
from concourse.alu_op_type import AluOpType as ALU
from contextlib import ExitStack
import math

FP32 = mybir.dt.float32
FP32R = mybir.dt.float32r
BF16 = mybir.dt.bfloat16
ACT = mybir.ActivationFunctionType
AX = mybir.AxisListType

PART = 128
BANK = 512
HEADS, DHEAD = 16, 64
EPS = 1e-5
CLIP = 11.0
SCALE = DHEAD ** -0.5
E_MIN, E_MAX = math.exp(-CLIP), math.exp(CLIP)


def xattn_moe_kernel(nc, x, ctx_1024, cos, sin, lat_g, lat_b, ctx_g, ctx_b, Wq, Wkv, Wo, bo, wg, W, b, out):
    BATCH, N, DIM = x.shape
    S = ctx_1024.shape[1]
    E = wg.shape[1]
    INNER = HEADS * DHEAD
    KT = DIM // PART
    NT = BATCH * N // PART
    NTB = N // PART
    ST = S // PART
    STA = BATCH * ST
    PAIRS = HEADS // 2
    PW = 2 * DHEAD
    PIECES = ST // 2
    CAP = BATCH * N // E
    assert BATCH == 2 and N == BANK and PW == PART and DIM == 256 and ST == 8

    x_v = x.rearrange("b (t p) d -> p (b t) d", p=PART)
    out_v = out.rearrange("b (t p) d -> p (b t) d", p=PART)
    ctx_v = ctx_1024.rearrange("b (t p) d -> p (b t) d", p=PART)
    cos_v = cos.rearrange("(t p) f -> p t f", p=PART)
    sin_v = sin.rearrange("(t p) f -> p t f", p=PART)
    Wq_v = Wq.rearrange("(k p) n -> p k n", p=PART)
    Wkv_v = Wkv.rearrange("(k p) (c n) -> p k c n", p=PART, c=2)
    Wo_v = Wo.rearrange("(r p) n -> p r n", p=PART)
    wg_v = wg.rearrange("(k p) e -> p k e", p=PART)
    W_v = W.rearrange("e (t p) h -> p (e t) h", p=PART)

    es = ExitStack()
    with es:
        def sb(name, shape, dt=FP32):
            return es.enter_context(nc.sbuf_tensor(name, shape, dt))

        def over(name, shape, place, dt=FP32):
            return nc.alloc_sbuf_tensor_at(name, shape, dt, offset=place)

        def sem(name):
            return es.enter_context(nc.semaphore(name))

        x_sb = sb("x_sb", [PART, NT, DIM])
        ctx_space = -(-nc.sbuf_base // 32) * 32
        ctxT_h = sb("ctxT_h", [PART, KT, STA * PART], FP32R)
        ctxT_l = sb("ctxT_l", [PART, KT, STA * PART], FP32R)
        x_space = -(-nc.sbuf_base // 32) * 32
        xT_h = sb("xT_h", [PART, KT, BATCH * N], FP32R)
        xT_l = sb("xT_l", [PART, KT, BATCH * N], FP32R)
        k_space = -(-nc.sbuf_base // 32) * 32
        k_stack = sb("k_stack", [PART, BATCH, 2, S], FP32R)
        q_high = sb("q_high", [PART, BATCH, 2, N], FP32R)
        q_low = sb("q_low", [PART, BATCH, 2, N], FP32R)
        v_space = -(-nc.sbuf_base // 32) * 32
        v_sb = sb("v_sb", [PART, BATCH, ST, PW])
        P_SLOTS = 4
        probs_space = -(-nc.sbuf_base // 32) * 32
        probs = sb("probs", [PART, P_SLOTS, 2, N])
        psum_acc = sb("psum_acc", [PART, BATCH, 2 * N])
        cosT = sb("cosT", [PART, ST, 2, 2, DHEAD // 2])
        sinT = sb("sinT", [PART, ST, 2, 2, DHEAD // 2])
        w_raw = sb("w_raw", [PART, KT, 3, PW])
        wkv_h = sb("wkv_h", [PART, KT, 2, PW], FP32R)
        wkv_l = sb("wkv_l", [PART, KT, 2, PW], FP32R)
        wq_h = sb("wq_h", [PART, KT, PW], FP32R)
        wq_l = sb("wq_l", [PART, KT, PW], FP32R)
        rope_a = sb("rope_a", [PART, 2, 2 * PW])
        rope_b = sb("rope_b", [PART, 2, 2 * PW])
        k_rot = sb("k_rot", [PART, 2, 2 * PW])
        k_nat = sb("k_nat", [PART, 2, 4, 2, DHEAD], FP32R)
        o_raw = sb("o_raw", [PART, BATCH, N])
        den_sb = sb("den_sb", [64, BATCH, N])
        den_t = sb("den_t", [PART, BATCH, 8])
        rden_t = sb("rden_t", [PART, BATCH, 8])
        rden_b = sb("rden_b", [PART, BATCH, N])
        attn_T = sb("attn_T", [PART, PAIRS, BATCH * N])
        wo_sb = sb("wo_sb", [PART, PAIRS, DIM])
        ident = sb("ident", [PART, PART])
        ones = sb("ones", [PART, 32])
        lng = sb("lng", [PART, 4, KT])
        bo_b = sb("bo_b", [PART, DIM])
        wg_sb = sb("wg_sb", [PART, KT, E])
        b_sb = sb("b_sb", [E, DIM])
        GR = NTB + ST
        bn = sb("bn", [PART, GR, 6])
        mv = sb("mv", [PART, GR, 2])
        var = sb("var", [PART, GR])
        std = sb("std", [PART, GR])
        rs_a = sb("rs_a", [PART, GR])
        rs_b = sb("rs_b", [PART, GR])
        rstd = sb("rstd", [PART, GR])
        ones_b = sb("ones_b", [PART, PART], BF16)
        upper_b = sb("upper_b", [PART, PART], BF16)
        rank_w = sb("rank_w", [PART, E])
        logit = sb("logit", [PART, NT, E])
        lmax = sb("lmax", [PART, NT])
        shifted = sb("shifted", [PART, NT, E])
        expd = sb("expd", [PART, NT, E])
        esum = sb("esum", [PART, NT])
        gate = sb("gate", [PART, NT])
        first = sb("first", [PART, NT, E])
        fmax = sb("fmax", [PART, NT])
        mask = sb("mask", [PART, NT, E])
        mask_b = sb("mask_b", [PART, NT, E], BF16)
        weight = sb("weight", [PART, NT, E])
        ctx_n = attn_T[:, 0:4, :].rearrange("p a (t d) -> p (a t) d", d=DIM)
        x_n = probs[:, :, :, :].rearrange("p a h (t d) -> p (a h t) d", d=DIM)[:, 0:NT, :]
        full = psum_acc[:, :, :].rearrange("p b (c n) -> p (b c) n", n=BANK)
        w_bytes, tile_bytes = 4 * KT * E * DIM, 4 * NT * DIM
        WT_h = over("WT_h", [PART, KT, E, DIM], ctx_space, FP32R)
        WT_l = over("WT_l", [PART, KT, E, DIM], ctx_space + w_bytes, FP32R)
        W_nat = over("W_nat", [PART, E * KT, DIM], x_space)
        weight_T = over("weight_T", [E, NT * PART], x_space)
        x_1 = over("x_1", [PART, NT, DIM], k_space)
        x_1n = over("x_1n", [PART, NT, DIM], k_space + tile_bytes)
        x_1T = over("x_1T", [PART, KT, NT * PART], k_space + 2 * tile_bytes)
        acc = over("acc", [PART, NT, DIM], k_space + 3 * tile_bytes)
        x_1Th = over("x_1Th", [PART, KT, NT * PART], v_space, FP32R)
        x_1Tl = over("x_1Tl", [PART, KT, NT * PART], probs_space, FP32R)
        acc_odd = over("acc_odd", [PART, 2, DIM], probs_space + tile_bytes)

        psum = es.enter_context(nc.psum_tensor("psum", [PART, 8, BANK], FP32))
        scores = [psum[:, 0:2, :], psum[:, 2:4, :]]
        PROJ = (4, 5)
        o_ps = psum[:, 6, :]
        den_ps = psum[:, 7, :]
        scratch = nc.dram_tensor("rden_scratch", [BATCH, 2 * N], FP32, kind="Internal").ap()

        x_loaded = [sem(f"x_loaded_{half}") for half in range(BATCH)]
        ctx_loaded = [sem(f"ctx_loaded_{half}") for half in range(BATCH)]
        consts_loaded = sem("consts_loaded")
        cs_loaded, tail_loaded, consts_made = sem("cs_loaded"), sem("tail_loaded"), sem("consts_made")
        dve_step = sem("dve_step")
        pool_step = sem("pool_step")
        var_ready, std_ready = sem("var_ready"), sem("std_ready")
        ctx_normed, x_normed = sem("ctx_normed"), sem("x_normed")
        turned, turned_full, turned_high, turned_low = sem("turned"), sem("turned_full"), sem("turned_high"), sem("turned_low")
        W_turned, W_high, W_low, W_loaded = sem("W_turned"), sem("W_high"), sem("W_low"), sem("W_loaded")
        w_loaded, w_high, w_split = sem("w_loaded"), sem("w_high"), sem("w_split")
        kv_done, kt_done, q_done, q_spread = sem("kv_done"), sem("kt_done"), sem("q_done"), sem("q_spread")
        v_copied, kt_copied, q_copied, q_split = sem("v_copied"), sem("kt_copied"), sem("q_copied"), sem("q_split")
        rope_terms, k_summed, k_high, k_ready = sem("rope_terms"), sem("k_summed"), sem("k_high"), sem("k_ready")
        s_done, exp_done, clipped, summed = sem("s_done"), sem("exp_done"), sem("clipped"), sem("summed")
        av_done, o_copied, den_done, den_copied = sem("av_done"), sem("o_copied"), sem("den_done"), sem("den_copied")
        den_turned, rden_made, rden_stored = sem("den_turned"), sem("rden_made"), sem("rden_stored")
        rden_spread, heads_normed = sem("rden_spread"), sem("heads_normed")
        bias_added = sem("bias_added")
        wo_part_done, wo_part_added = sem("wo_part_done"), sem("wo_part_added")
        wo_done, x1_made, x1n_made = sem("wo_done"), sem("x1_made"), sem("x1n_made")
        x1_turned, x1T_copied, x1T_high, x1T_low = sem("x1_turned"), sem("x1T_copied"), sem("x1T_high"), sem("x1T_low")
        logits_done = sem("logits_done")
        shifted_made, expd_made, mask_made = sem("shifted_made"), sem("expd_made"), sem("mask_made")
        ranks_done, weight_made, weight_turned = sem("ranks_done"), sem("weight_made"), sem("weight_turned")
        weightT_copied, bias_done, tile_made = sem("weightT_copied"), sem("bias_done"), sem("tile_made")
        ffn_done, ffn_added, out_stored = sem("ffn_done"), sem("ffn_added"), sem("out_stored")

        UNITS = 2 * PAIRS
        last_unit = UNITS - 1
        TURNS = KT * (ST // 4 + 1)
        TURN_BANKS = (0, 1, 2, 3, 6, 7)

        def above_zero(value):
            return not isinstance(value, int) or value > 0

        def turn_group(half, g):
            t4, k = divmod(g, KT)
            if t4 < ST // 4:
                t0 = half * ST + 4 * t4
                cols = slice(t0 * PART, (t0 + 4) * PART)
                return ctx_n, t0, k, ctxT_h[:, k, cols], ctxT_l[:, k, cols], 2
            t0 = half * NTB
            cols = slice(t0 * PART, (t0 + 4) * PART)
            return x_n, t0, k, xT_h[:, k, cols], xT_l[:, k, cols], 0

        def kv_bank(p):
            return 0 if p == 0 else 1

        block = es.enter_context(nc.Block())

        @block.sync
        def _(sp):
            for half in range(BATCH):
                sp.dma_start(x_sb[:, half * NTB:(half + 1) * NTB, :], x_v[:, half * NTB:(half + 1) * NTB, :]).then_inc(x_loaded[half], 16)
                for h in range(2 * half, 2 * half + 2):
                    sp.dma_start(ctx_n[:, 4 * h:4 * h + 4, :], ctx_v[:, 4 * h:4 * h + 4, :]).then_inc(ctx_loaded[half], 16)

            def count(value):
                return value if isinstance(value, int) else sp.snap(sp.to_reg(value))

            sp.dma_start(w_raw[:, :, 0, :], Wq_v[:, :, 0:PW]).then_inc(w_loaded, 16)
            for c in range(2):
                sp.dma_start(w_raw[:, :, 1 + c, :], Wkv_v[:, :, c, 0:PW]).then_inc(w_loaded, 16)
            for h in range(2):
                sp.dma_start(cosT[:, :, h, 0, :], cos_v).then_inc(cs_loaded, 16)
                sp.dma_start(cosT[:, :, h, 1, :], cos_v).then_inc(cs_loaded, 16)
                sp.dma_start(sinT[:, :, h, 0, :], sin_v).then_inc(cs_loaded, 16)
                sp.dma_start(sinT[:, :, h, 1, :], sin_v).then_inc(cs_loaded, 16)
            sp.dma_start(wo_sb[:, :, :], Wo_v).then_inc(tail_loaded, 16)
            sp.dma_start(wg_sb[:, :, :], wg_v).then_inc(tail_loaded, 16)
            sp.dma_start(b_sb[:, :], b).then_inc(tail_loaded, 16)

            def sum_counts(u):
                return count(u - 1), count(u + 1), count(16 * (u + 1))

            def spread_sums(counts, b_):
                before, done, stored = counts
                sp.wait_ge(den_copied, done)
                for h in range(2):
                    sp.dma_start(den_t[64 * h:64 * h + 64, b_, :], den_sb[32 * h:32 * h + 1, b_, :]).then_inc(den_turned, 16)
                sp.wait_ge(rden_made, done)
                sp.dma_start(scratch[b_, :].rearrange("(p c) -> p c", c=8), rden_t[:, b_, :]).then_inc(rden_stored, 16)
                sp.wait_ge(rden_stored, stored)
                if above_zero(before):
                    sp.wait_ge(heads_normed, before)
                for h in range(2):
                    sp.dma_start(rden_b[64 * h:64 * h + 64, b_, :],
                                 scratch[b_:b_ + 1, h * N:(h + 1) * N].broadcast_to([64, N])).then_inc(rden_spread, 16)

            def spread_queries(done, bw):
                for parts, written in ((q_high, q_copied), (q_low, q_split)):
                    sp.wait_ge(written, done)
                    for h in range(2):
                        sp.dma_start(parts[(1 - h) * DHEAD:(2 - h) * DHEAD, bw, h, :].bitcast(FP32),
                                     parts[h * DHEAD:(h + 1) * DHEAD, bw, h, :].bitcast(FP32)).then_inc(q_spread, 16)

            def iteration(i, first=False):
                if not first:
                    sums_1 = sum_counts(2 * i - 1)
                queries_1 = count(4 * i + 4)
                sums_0 = sum_counts(2 * i)
                queries_0 = count(4 * i + 6)
                cols = bass.ds(count((i + 1) * PW), PW)
                sp.dma_start(w_raw[:, :, 0, :], Wq_v[:, :, cols]).then_inc(w_loaded, 16)
                for c in range(2):
                    sp.dma_start(w_raw[:, :, 1 + c, :], Wkv_v[:, :, c, cols]).then_inc(w_loaded, 16)
                spread_queries(queries_1, 1)
                if not first:
                    spread_sums(sums_1, 1)
                spread_queries(queries_0, 0)
                spread_sums(sums_0, 0)

            spread_queries(2, 0)
            iteration(0, first=True)
            with sp.Fori(1, PAIRS - 1) as i:
                iteration(i)
            spread_queries(2 * UNITS, 1)
            sp.dma_start(W_nat[:, :, :], W_v).then_inc(W_loaded, 16)
            spread_sums(sum_counts(last_unit - 2), 1)
            spread_sums(sum_counts(last_unit - 1), 0)
            spread_sums(sum_counts(last_unit), 1)
            for t in range(1, NT, 2):
                sp.wait_ge(tile_made, t + 1)
                sp.dma_start(out_v[:, t - 1:t + 1, :], acc[:, t - 1:t + 1, :]).then_inc(out_stored, 16)
            sp.wait_ge(out_stored, 16 * (NT // 2))

        @block.gpsimd
        def _(pool):
            steps = [0]

            def then(ins):
                steps[0] += 1
                ins.then_inc(pool_step, 1)
                pool.wait_ge(pool_step, steps[0])

            then(nc.gpsimd.memset(ident[:, :], 0.0))
            nc.gpsimd.affine_select(out=ident[:, :], in_=ident[:, :], compare_op=ALU.not_equal, fill=1.0, base=0,
                                    pattern=[[-1, PART]], channel_multiplier=1).then_inc(consts_made, 1)
            nc.gpsimd.memset(ones[:, :], 1.0).then_inc(consts_made, 1)
            with nc.allow_non_contiguous_dma(reason="256 values each"):
                for n, v in enumerate((lat_g, lat_b, ctx_g, ctx_b)):
                    pool.dma_start(lng[:, n, :], v.rearrange("(k p) -> p k", p=PART)).then_inc(consts_loaded, 16)
            pool.dma_start(bo_b[:, :], bo.rearrange("(o n) -> o n", o=1).broadcast_to([PART, DIM])).then_inc(consts_loaded, 16)

            one = ones[:, 0:1].unsqueeze(2).unsqueeze(3)

            def split_pair(i):
                pool.wait_ge(w_loaded, 48 * (i + 1))
                if above_zero(i):
                    pool.wait_ge(kv_done, 2 * PIECES * i)
                nc.gpsimd.tensor_tensor(wkv_h[:, :, :, :], w_raw[:, :, 1:3, :], one.broadcast_to([PART, KT, 2, PW]),
                                        ALU.mult).then_inc(w_high, 1)
                nc.gpsimd.tensor_copy(wq_h[:, :, :], w_raw[:, :, 0, :]).then_inc(w_high, 1)
                pool.wait_ge(w_high, 2 * (i + 1))
                nc.gpsimd.tensor_tensor(wkv_l[:, :, :, :], w_raw[:, :, 1:3, :], wkv_h[:, :, :, :].bitcast(FP32),
                                        ALU.subtract).then_inc(w_split, 1)
                nc.gpsimd.tensor_tensor(wq_l[:, :, :], w_raw[:, :, 0, :], wq_h[:, :, :].bitcast(FP32),
                                        ALU.subtract).then_inc(w_split, 1)

            pool.wait_ge(consts_made, 2)
            def low_keys(w, p):
                t = PIECES * w + p
                pool.wait_ge(k_high, t + 1)
                nc.gpsimd.tensor_tensor(k_nat[:, p % 2, :, 1, :], k_rot[:, p % 2, :].rearrange("p (a d) -> p a d", a=4),
                                        k_nat[:, p % 2, :, 0, :].bitcast(FP32), ALU.subtract).then_inc(k_ready, 1)

            def iteration(i):
                for p in range(PIECES):
                    low_keys(2 * i + 1, p)
                split_pair(i + 1)
                for p in range(PIECES):
                    low_keys(2 * i + 2, p)

            split_pair(0)
            nc.gpsimd.memset(ones_b[:, :], 1.0).then_inc(consts_made, 1)
            then(nc.gpsimd.memset(upper_b[:, :], 0.0))
            nc.gpsimd.affine_select(out=upper_b[:, :], in_=upper_b[:, :], compare_op=ALU.is_ge, fill=1.0, base=0,
                                    pattern=[[-1, PART]], channel_multiplier=1).then_inc(consts_made, 1)
            for e in range(E):
                last = nc.gpsimd.memset(rank_w[:, e:e + 1], float(E - e))
            last.then_inc(consts_made, 1)
            for p in range(PIECES):
                low_keys(0, p)
            pool.wait_ge(x_normed, 2 * BATCH)
            pool.wait_ge(consts_loaded, 80)
            for t in range(NT):
                last = nc.gpsimd.tensor_tensor(x_sb[:, t, :], x_sb[:, t, :], bo_b[:, :], ALU.add)
            last.then_inc(bias_added, 1)
            iteration(0)
            with pool.Fori(1, PAIRS - 1) as i:
                iteration(i)
            for p in range(PIECES):
                low_keys(last_unit, p)

        @block.scalar
        def _(act):
            def inverse_roots(n, sl):
                act.wait_ge(var_ready, n)
                nc.scalar.activation(std[:, sl], var[:, sl], ACT.Sqrt).then_inc(std_ready, 1)

            def scale_turned(half, g):
                _, _, k, _, _, c = turn_group(half, g)
                n = half * TURNS + g
                act.wait_ge(turned, n + 1)
                if n >= 4:
                    act.wait_ge(turned_low, n - 3)
                nc.scalar.activation(full[:, n % 4, :], psum[:, TURN_BANKS[g], :], ACT.Identity, scale=lng[:, c, k:k + 1],
                                     bias=lng[:, c + 1, k:k + 1]).then_inc(turned_full, 1)

            def high_W(g):
                ep, k = divmod(g, KT)
                act.wait_ge(W_turned, g + 1)
                nc.scalar.copy(WT_h[:, k, 2 * ep:2 * ep + 2, :],
                               psum[:, g % 4, :].rearrange("p (e f) -> p e f", e=2)).then_inc(W_high, 1)

            def copy_v(w, bw, p):
                act.wait_ge(kv_done, PIECES * w + p + 1)
                nc.scalar.copy(v_sb[:, bw, 2 * p:2 * p + 2, :],
                               psum[:, PROJ[kv_bank(p)], 2 * PW:4 * PW].rearrange("p (t n) -> p t n", t=2)).then_inc(v_copied, 1)

            def high_keys(w, p):
                t = PIECES * w + p
                act.wait_ge(k_summed, t + 1)
                if above_zero(t - 1):
                    act.wait_ge(kt_done, t - 1)
                nc.scalar.copy(k_nat[:, p % 2, :, 0, :], k_rot[:, p % 2, :].rearrange("p (a d) -> p a d", a=4)).then_inc(k_high, 1)

            def copy_kt(w, bw, p):
                act.wait_ge(kt_done, PIECES * w + p + 1)
                nc.scalar.copy(k_stack[:, bw, :, 2 * p * PART:(2 * p + 2) * PART],
                               psum[:, PROJ[0], :].rearrange("p (h s) -> p h s", h=2)).then_inc(kt_copied, 1)

            def copy_q(w, bw):
                act.wait_ge(q_done, w + 1)
                for h in range(2):
                    rows = slice(h * DHEAD, (h + 1) * DHEAD)
                    nc.scalar.copy(q_high[rows, bw, h, :], psum[rows, PROJ[1], :]).then_inc(q_copied, 1)

            def copy_o(u, b_):
                act.wait_ge(av_done, ST * (u + 1))
                if above_zero(u - 1):
                    act.wait_ge(heads_normed, u - 1)
                nc.scalar.copy(o_raw[:, b_, :], o_ps).then_inc(o_copied, 1)

            def copy_den(u, b_):
                act.wait_ge(den_done, u + 1)
                if above_zero(u - 1):
                    act.wait_ge(den_turned, 32 * (u - 1))
                nc.scalar.copy(den_sb[:, b_, :], den_ps[0:64, :]).then_inc(den_copied, 1)

            def unit(u, b_, before=True, after=True):
                w, bw = u + 1, 1 - b_
                for j in range(ST):
                    c = ST * u + j
                    act.wait_ge(s_done, c + 1)
                    if above_zero(c - P_SLOTS + 1):
                        act.wait_ge(av_done, c - P_SLOTS + 1)
                        jp = (j - P_SLOTS) % ST
                        act.wait_ge(summed, (ST - 1) * (u if j >= P_SLOTS else u - 1) + max(jp, 1))
                    nc.scalar.activation(probs[:, j % P_SLOTS, :, :], scores[j % 2], ACT.Exp, scale=SCALE).then_inc(exp_done, 1)
                    if before and j == 1:
                        copy_o(u - 1, bw)
                    if before and j == 2:
                        copy_den(u - 1, bw)
                    if after:
                        if j == 0:
                            copy_q(w, bw)
                        if 1 <= j < 1 + PIECES:
                            high_keys(w, j - 1)
                        if j < PIECES:
                            copy_v(w, bw, j)
                        if 2 <= j < 2 + PIECES:
                            copy_kt(w, bw, j - 2)

            inverse_roots(1, slice(0, GR))
            inverse_roots(2, slice(0, NTB))
            act.wait_ge(consts_loaded, 80)
            for g in range(TURNS):
                scale_turned(0, g)
            inverse_roots(3, slice(0, GR))
            copy_q(0, 0)
            copy_v(0, 0, 0)
            copy_v(0, 0, 1)
            high_keys(0, 0)
            inverse_roots(4, slice(0, NTB))
            for p in range(2, PIECES):
                copy_kt(0, 0, p - 2)
                high_keys(0, p - 1)
                copy_v(0, 0, p)
            high_keys(0, PIECES - 1)
            copy_kt(0, 0, 2)
            copy_kt(0, 0, 3)
            for g in range(TURNS):
                scale_turned(1, g)
            unit(0, 0, before=False)
            unit(1, 1)
            with act.Fori(1, PAIRS - 1) as i:
                unit(2 * i, 0)
                unit(2 * i + 1, 1)
            unit(last_unit - 1, 0)
            unit(last_unit, 1, after=False)
            copy_o(last_unit, 1)
            copy_den(last_unit, 1)

            def roots_x1(g):
                inverse_roots(5 + g, slice(g * NTB, (g + 1) * NTB))

            def copy_x1T(g):
                cols = slice(g * N, (g + 1) * N)
                for k in range(KT):
                    act.wait_ge(x1_turned, KT * g + k + 1)
                    nc.scalar.copy(x_1T[:, k, cols], psum[:, 4 + 2 * g + k, :]).then_inc(x1T_copied, 1)
                for k in range(KT):
                    act.wait_ge(x1T_copied, KT * g + k + 1)
                    nc.scalar.copy(x_1Th[:, k, cols], x_1T[:, k, cols]).then_inc(x1T_high, 1)

            def exp_logits(g):
                ts = slice(g * NTB, (g + 1) * NTB)
                act.wait_ge(shifted_made, g + 1)
                nc.scalar.activation(expd[:, ts, :], shifted[:, ts, :], ACT.Exp).then_inc(expd_made, 1)

            def copy_weightT(g):
                act.wait_ge(weight_turned, g + 1)
                nc.scalar.copy(weight_T[:, g * N:(g + 1) * N], psum[0:E, 4 + 2 * g, :]).then_inc(weightT_copied, 1)

            for g in range(E // 2):
                high_W(g)
            roots_x1(0)
            copy_x1T(0)
            for g in range(E // 2, E):
                high_W(g)
            exp_logits(0)
            roots_x1(1)
            copy_weightT(0)
            copy_x1T(1)
            exp_logits(1)
            copy_weightT(1)

        @block.vector
        def _(dve):
            steps = [0]

            def then(ins):
                steps[0] += 1
                ins.then_inc(dve_step, 1)
                dve.wait_ge(dve_step, steps[0])

            def inverse_std(sl, ready):
                dve.wait_ge(std_ready, ready)
                then(nc.vector.reciprocal(rs_a[:, sl], std[:, sl]))
                then(nc.vector.tensor_tensor(rs_b[:, sl], rs_a[:, sl], rs_a[:, sl], ALU.mult))
                then(nc.vector.tensor_tensor(rs_b[:, sl], rs_b[:, sl], var[:, sl], ALU.mult))
                then(nc.vector.tensor_scalar(rs_b[:, sl], rs_b[:, sl], -0.5, 1.5, ALU.mult, ALU.add))
                then(nc.vector.tensor_tensor(rstd[:, sl], rs_a[:, sl], rs_b[:, sl], ALU.mult))

            def stats(tiles, at):
                for t in range(tiles.shape[1]):
                    last = nc.vector.bn_stats(bn[:, at + t, :], tiles[:, t, :])
                then(last)
                for t in range(tiles.shape[1]):
                    last = nc.vector.bn_aggr(mv[:, at + t, :], bn[:, at + t, :])
                then(last)

            def add_eps(sl):
                nc.vector.tensor_scalar(var[:, sl], mv[:, sl, 1], EPS, None, ALU.add).then_inc(var_ready, 1)

            def normalise(dst, src, t, at):
                return nc.vector.tensor_scalar(dst[:, t, :], src[:, t, :], mv[:, at + t, 0:1], rstd[:, at + t:at + t + 1],
                                               ALU.subtract, ALU.mult)

            def x_stats(half):
                dve.wait_ge(x_loaded[half], 16)
                stats(x_sb[:, half * NTB:(half + 1) * NTB, :], 0)

            def ctx_stats(half):
                dve.wait_ge(ctx_loaded[half], 32)
                stats(ctx_n[:, half * ST:(half + 1) * ST, :], NTB)
                add_eps(slice(0, GR))

            def normalise_rows(half):
                x0, c0 = half * NTB, half * ST
                inverse_std(slice(0, GR), 2 * half + 1)
                for t in range(NTB):
                    last = normalise(x_n, x_sb, x0 + t, -x0)
                then(last)
                for t in range(ST):
                    normalise(ctx_n, ctx_n, c0 + t, NTB - c0).then_inc(ctx_normed, 1)
                stats(x_n[:, x0:x0 + NTB, :], 0)
                add_eps(slice(0, NTB))
                inverse_std(slice(0, NTB), 2 * half + 2)
                for t in range(NTB):
                    last = normalise(x_n, x_n, x0 + t, -x0)
                last.then_inc(x_normed, 2)

            def split_turned(half, g):
                _, _, _, high, low, _ = turn_group(half, g)
                n = half * TURNS + g
                dve.wait_ge(turned_full, n + 1)
                nc.vector.tensor_copy(high, full[:, n % 4, :]).then_inc(turned_high, 1)
                dve.wait_ge(turned_high, n + 1)
                nc.vector.tensor_tensor(low, full[:, n % 4, :], high.bitcast(FP32), ALU.subtract).then_inc(turned_low, 1)

            def rope(w, p):
                t = PIECES * w + p
                src = psum[:, PROJ[kv_bank(p)], 0:2 * PW].rearrange("p (a f c) -> p a f c", f=2, c=DHEAD // 2)
                cosv = cosT[:, 2 * p:2 * p + 2, :, :, :].rearrange("p t h f c -> p (t h) f c")
                sinv = sinT[:, 2 * p:2 * p + 2, :, :, :].rearrange("p t h f c -> p (t h) f c")
                a, bb, kr = rope_a[:, p % 2, :], rope_b[:, p % 2, :], k_rot[:, p % 2, :]
                a4 = a.rearrange("p (a f c) -> p a f c", f=2, c=DHEAD // 2)
                b4 = bb.rearrange("p (a f c) -> p a f c", f=2, c=DHEAD // 2)
                dve.wait_ge(v_copied, t + 1)
                nc.vector.tensor_tensor(a4, src, cosv, ALU.mult).then_inc(rope_terms, 1)
                nc.vector.tensor_tensor(b4, src[:, :, ::-1, :], sinv, ALU.mult).then_inc(rope_terms, 1)
                dve.wait_ge(rope_terms, 2 * (t + 1))
                if above_zero(t - 1):
                    dve.wait_ge(k_ready, t - 1)
                nc.vector.tensor_tensor(kr, a, bb, ALU.add).then_inc(k_summed, 1)

            def split_q(w, bw):
                dve.wait_ge(q_copied, 2 * (w + 1))
                for h in range(2):
                    rows = slice(h * DHEAD, (h + 1) * DHEAD)
                    nc.vector.tensor_tensor(q_low[rows, bw, h, :], psum[rows, PROJ[1], :], q_high[rows, bw, h, :].bitcast(FP32),
                                            ALU.subtract).then_inc(q_split, 1)

            def invert_sums(u, b_):
                dve.wait_ge(den_turned, 32 * (u + 1))
                if above_zero(u - 1):
                    dve.wait_ge(rden_stored, 16 * (u - 1))
                nc.vector.reciprocal(rden_t[:, b_, :], den_t[:, b_, :]).then_inc(rden_made, 1)

            def norm_heads(i, u, b_):
                dve.wait_ge(rden_spread, 32 * (u + 1))
                dve.wait_ge(o_copied, u + 1)
                dst = attn_T[:, bass.ds(i, 1), b_ * N:(b_ + 1) * N].rearrange("p o n -> p (o n)")
                nc.vector.tensor_tensor(dst, o_raw[:, b_, :], rden_b[:, b_, :], ALU.mult).then_inc(heads_normed, 1)

            def add_part(t):
                dve.wait_ge(wo_part_done, t - t % 2 + 2)
                nc.vector.tensor_tensor(x_sb[:, t, :], psum[:, 4 + t // 2, (t % 2) * DIM:(t % 2 + 1) * DIM],
                                        x_sb[:, t, :], ALU.add).then_inc(wo_part_added, 1)

            def unit(i, u, b_, before=1, after=True):
                w, bw = u + 1, 1 - b_
                for j in range(ST):
                    c = ST * u + j
                    chunk = probs[:, j % P_SLOTS, :, :].rearrange("p h n -> p (h n)")
                    dve.wait_ge(exp_done, c + 1)
                    nc.vector.tensor_scalar(chunk, chunk, E_MIN, E_MAX, ALU.max, ALU.min).then_inc(clipped, 1)
                    if j >= 1:
                        dve.wait_ge(clipped, c + 1)
                        if j == 1 and before >= 2:
                            dve.wait_ge(den_done, u - 1)
                        if j >= 2:
                            dve.wait_ge(summed, (ST - 1) * u + j - 1)
                        prev = probs[:, 0, :, :].rearrange("p h n -> p (h n)") if j == 1 else psum_acc[:, b_, :]
                        nc.vector.tensor_tensor(psum_acc[:, b_, :], prev, chunk, ALU.add).then_inc(summed, 1)
                    if j == 1 and before >= 2:
                        norm_heads(i - 1, u - 2, b_)
                    if not after and j % 2:
                        add_part(j // 2)
                    if after and j == 0:
                        split_q(w, bw)
                    if after and j < PIECES:
                        rope(w, j)
                    if j == 4 and before >= 1:
                        invert_sums(u - 1, bw)

            x_stats(0)
            ctx_stats(0)
            normalise_rows(0)
            for g in range(TURNS):
                split_turned(0, g)
            dve.wait_ge(cs_loaded, 128)
            then(nc.vector.tensor_scalar(sinT[:, :, :, 0, :], sinT[:, :, :, 0, :], -1.0, None, ALU.mult))
            x_stats(1)
            ctx_stats(1)
            split_q(0, 0)
            rope(0, 0)
            rope(0, 1)
            normalise_rows(1)
            rope(0, 2)
            rope(0, 3)
            for g in range(TURNS):
                split_turned(1, g)
            unit(0, 0, 0, before=0)
            unit(0, 1, 1, before=1)
            with dve.Fori(1, PAIRS - 1) as i:
                unit(i, 2 * i, 0, before=2)
                unit(i, 2 * i + 1, 1, before=2)
            unit(PAIRS - 1, last_unit - 1, 0, before=2)
            unit(PAIRS - 1, last_unit, 1, before=2, after=False)
            norm_heads(PAIRS - 1, last_unit - 1, 0)

            def slices(g):
                return slice(g * NTB, (g + 1) * NTB), range(g * NTB, (g + 1) * NTB)

            def x1_stats(g):
                ts, tiles = slices(g)
                for t in tiles:
                    dve.wait_ge(wo_done, t - t % 2 + 2)
                    nc.vector.tensor_tensor(x_1[:, t, :], psum[:, 4 + t // 2, (t % 2) * DIM:(t % 2 + 1) * DIM],
                                            x_sb[:, t, :], ALU.add).then_inc(x1_made, 1)
                dve.wait_ge(x1_made, (g + 1) * NTB)
                stats(x_1[:, ts, :], g * NTB)
                add_eps(ts)

            def x1_normalise(g):
                ts, tiles = slices(g)
                inverse_std(ts, 5 + g)
                for t in tiles:
                    normalise(x_1n, x_1, t, 0).then_inc(x1n_made, 1)

            def low_W(g):
                ep, k = divmod(g, KT)
                dve.wait_ge(W_high, g + 1)
                nc.vector.tensor_tensor(WT_l[:, k, 2 * ep:2 * ep + 2, :], psum[:, g % 4, :].rearrange("p (e f) -> p e f", e=2),
                                        WT_h[:, k, 2 * ep:2 * ep + 2, :].bitcast(FP32), ALU.subtract).then_inc(W_low, 1)

            def low_x1T(g):
                cols = slice(g * N, (g + 1) * N)
                for k in range(KT):
                    dve.wait_ge(x1T_high, KT * g + k + 1)
                    nc.vector.tensor_tensor(x_1Tl[:, k, cols], x_1T[:, k, cols], x_1Th[:, k, cols].bitcast(FP32),
                                            ALU.subtract).then_inc(x1T_low, 1)

            def choose(g):
                ts, _ = slices(g)
                dve.wait_ge(logits_done, g + 1)
                then(nc.vector.tensor_copy(logit[:, ts, :], psum[:, 4 + 2 * g, 0:NTB * E].rearrange("p (t e) -> p t e", e=E)))
                then(nc.vector.reduce_max(lmax[:, ts], logit[:, ts, :], AX.X))
                nc.vector.tensor_tensor(shifted[:, ts, :], logit[:, ts, :], lmax[:, ts].unsqueeze(2).broadcast_to([PART, NTB, E]),
                                        ALU.subtract).then_inc(shifted_made, 1)
                dve.wait_ge(shifted_made, g + 1)
                dve.wait_ge(consts_made, 5)
                then(nc.vector.scalar_tensor_tensor(out=first[:, ts, :], in0=shifted[:, ts, :], scalar=0.0,
                                                    in1=rank_w[:, :].unsqueeze(1).broadcast_to([PART, NTB, E]),
                                                    op0=ALU.is_equal, op1=ALU.mult))
                then(nc.vector.reduce_max(fmax[:, ts], first[:, ts, :], AX.X))
                then(nc.vector.tensor_tensor(mask[:, ts, :], first[:, ts, :], fmax[:, ts].unsqueeze(2).broadcast_to([PART, NTB, E]),
                                             ALU.is_equal))
                nc.vector.tensor_copy(mask_b[:, ts, :], mask[:, ts, :]).then_inc(mask_made, 1)
                dve.wait_ge(expd_made, g + 1)
                then(nc.vector.reduce_sum(esum[:, ts], expd[:, ts, :], AX.X))
                then(nc.vector.reciprocal(gate[:, ts], esum[:, ts]))

            def weigh_tokens(g):
                ts, _ = slices(g)
                dve.wait_ge(ranks_done, g + 1)
                then(nc.vector.scalar_tensor_tensor(out=weight[:, ts, :],
                                                    in0=psum[:, 5 + 2 * g, 0:NTB * E].rearrange("p (t e) -> p t e", e=E),
                                                    scalar=float(CAP), in1=mask[:, ts, :], op0=ALU.is_lt, op1=ALU.mult))
                nc.vector.tensor_tensor(weight[:, ts, :], weight[:, ts, :], gate[:, ts].unsqueeze(2).broadcast_to([PART, NTB, E]),
                                        ALU.mult).then_inc(weight_made, 1)
                dve.wait_ge(weight_made, g + 1)

            def add_experts(t):
                odd = acc_odd[:, t % 2, :]
                for e in range(E):
                    out_e = psum[:, e // 2, (e % 2) * DIM:(e % 2 + 1) * DIM]
                    w_e = weight[:, t, e:e + 1]
                    dve.wait_ge(ffn_done, (t * E + e) // 2 + 1)
                    if e == 1:
                        nc.vector.tensor_scalar(odd, out_e, w_e, None, ALU.mult).then_inc(ffn_added, 1)
                        continue
                    if e >= 2:
                        dve.wait_ge(ffn_added, t * E + e - 1)
                    sum_ = odd if e % 2 else acc[:, t, :]
                    nc.vector.scalar_tensor_tensor(out=sum_, in0=out_e, scalar=w_e, in1=sum_ if e else x_1[:, t, :],
                                                   op0=ALU.mult, op1=ALU.add).then_inc(ffn_added, 1)
                dve.wait_ge(ffn_added, (t + 1) * E)
                then(nc.vector.tensor_tensor(acc[:, t, :], acc[:, t, :], odd, ALU.add))

            def add_bias(t):
                dve.wait_ge(bias_done, t - t % 2 + 2)
                nc.vector.tensor_tensor(acc[:, t, :], psum[:, 4 + t // 2, (t % 2) * DIM:(t % 2 + 1) * DIM],
                                        acc[:, t, :], ALU.add).then_inc(tile_made, 1)

            dve.wait_ge(bias_added, 1)
            x1_stats(0)
            invert_sums(last_unit, 1)
            x1_normalise(0)
            for g in range(E // 2):
                low_W(g)
            for n in range(2):
                add_part(NTB + n)
            for g in range(E // 2, E):
                low_W(g)
            norm_heads(PAIRS - 1, last_unit, 1)
            low_x1T(0)
            for n in range(2, NTB):
                add_part(NTB + n)
            choose(0)
            x1_stats(1)
            x1_normalise(1)
            weigh_tokens(0)
            add_experts(0)
            low_x1T(1)
            add_experts(1)
            add_bias(0)
            add_bias(1)
            add_experts(2)
            choose(1)
            add_bias(2)
            add_experts(3)
            weigh_tokens(1)
            add_bias(3)
            add_experts(4)
            add_experts(5)
            add_bias(4)
            add_bias(5)
            for t in range(6, NT):
                add_experts(t)
                add_bias(t)

        @block.tensor
        def _(pe):
            def turn_rows(half, g):
                src, t0, k, _, _, _ = turn_group(half, g)
                if src is ctx_n:
                    pe.wait_ge(ctx_normed, t0 + 4)
                else:
                    pe.wait_ge(x_normed, 2 * (half + 1))
                if half:
                    pe.wait_ge(turned_full, g + 1)
                for n in range(4):
                    last = nc.tensor.transpose(psum[:, TURN_BANKS[g], n * PART:(n + 1) * PART],
                                               src[:, t0 + n, k * PART:(k + 1) * PART], ident[:, :])
                last.then_inc(turned, 1)

            def project_kv(w, bw, p):
                if p == 0:
                    if above_zero(PIECES * w):
                        pe.wait_ge(kt_copied, PIECES * w)
                elif p == 1:
                    pe.wait_ge(q_split, 2 * (w + 1))
                else:
                    pe.wait_ge(rope_terms, 2 * (PIECES * w + p))
                bank = psum[:, PROJ[kv_bank(p)], :].rearrange("p (c t n) -> p c t n", c=2, t=2)
                for t in range(2):
                    cols = slice((bw * ST + 2 * p + t) * PART, (bw * ST + 2 * p + t + 1) * PART)
                    terms = [(a, w_) for k in range(KT) for a, w_ in
                             ((ctxT_h[:, k, cols], wkv_h[:, k, :, :]), (ctxT_h[:, k, cols], wkv_l[:, k, :, :]),
                              (ctxT_l[:, k, cols], wkv_h[:, k, :, :]))]
                    for n, (a, w_) in enumerate(terms):
                        last = nc.tensor.matmul(bank[:, :, t, :], a, w_, start=(n == 0), stop=(n == len(terms) - 1))
                last.then_inc(kv_done, 1)

            def turn_keys(w, p):
                pe.wait_ge(k_ready, PIECES * w + p + 1)
                if p > 0:
                    pe.wait_ge(kt_copied, PIECES * w + p)
                for h in range(2):
                    for t in range(2):
                        last = nc.tensor.transpose(psum[:, PROJ[0], (2 * h + t) * PART:(2 * h + t + 1) * PART],
                                                   k_nat[:, p % 2, 2 * t + h, :, :].rearrange("p a d -> p (a d)").bitcast(FP32),
                                                   ident[:, :])
                last.then_inc(kt_done, 1)

            def project_q(i, w, bw):
                pe.wait_ge(w_split, 2 * (i + 1))
                if above_zero(w):
                    pe.wait_ge(rope_terms, 2 * PIECES * w)
                cols = slice(bw * N, (bw + 1) * N)
                terms = [(w_, a) for k in range(KT) for w_, a in
                         ((wq_h[:, k, :], xT_h[:, k, cols]), (wq_h[:, k, :], xT_l[:, k, cols]),
                          (wq_l[:, k, :], xT_h[:, k, cols]))]
                for n, (w_, a) in enumerate(terms):
                    last = nc.tensor.matmul(psum[:, PROJ[1], :], w_, a, start=(n == 0), stop=(n == len(terms) - 1))
                last.then_inc(q_done, 1)

            def score(u, b_, j):
                c = ST * u + j
                if j == 0:
                    pe.wait_ge(kt_copied, PIECES * (u + 1))
                    pe.wait_ge(q_split, 2 * (u + 1))
                    pe.wait_ge(q_spread, 64 * (u + 1))
                if above_zero(c - 1):
                    pe.wait_ge(exp_done, c - 1)
                for h in range(2):
                    keys = k_stack[:, b_, h, j * PART:(j + 1) * PART]
                    nc.tensor.matmul(scores[j % 2][:, h, :], keys, q_high[:, b_, h, :], start=True, stop=False)
                    last = nc.tensor.matmul(scores[j % 2][:, h, :], keys, q_low[:, b_, h, :], start=False, stop=True)
                last.then_inc(s_done, 1)

            def weigh_values(u, b_, j):
                if j == 0:
                    pe.wait_ge(v_copied, PIECES * (u + 1))
                    if above_zero(u):
                        pe.wait_ge(o_copied, u)
                pe.wait_ge(clipped, ST * u + j + 1)
                for h in range(2):
                    last = nc.tensor.matmul(o_ps[64 * h:64 * h + 64, :], v_sb[:, b_, j, h * DHEAD:(h + 1) * DHEAD],
                                            probs[:, j % P_SLOTS, h, :], start=(j == 0), stop=(j == ST - 1))
                last.then_inc(av_done, 1)

            def sum_probs(u, b_):
                pe.wait_ge(summed, (ST - 1) * (u + 1))
                if above_zero(u):
                    pe.wait_ge(den_copied, u)
                for h in range(2):
                    last = nc.tensor.matmul(den_ps[32 * h:32 * h + 32, :], ones[:, :], psum_acc[:, b_, h * N:(h + 1) * N],
                                            start=True, stop=True)
                last.then_inc(den_done, 1)

            def turn_W(g):
                ep, k = divmod(g, KT)
                if g == 0:
                    pe.wait_ge(exp_done, ST * UNITS)
                    pe.wait_ge(W_loaded, 16)
                if g >= 4:
                    pe.wait_ge(W_low, g - 3)
                for n in range(4):
                    last = nc.tensor.transpose(psum[:, g % 4, n * PART:(n + 1) * PART],
                                               W_nat[:, 4 * ep + n, k * PART:(k + 1) * PART], ident[:, :])
                last.then_inc(W_turned, 1)

            def out_half(t):
                return psum[:, 4 + t // 2, (t % 2) * DIM:(t % 2 + 1) * DIM]

            def wo_part(t):
                for r in range(PAIRS - 1):
                    last = nc.tensor.matmul(out_half(t), attn_T[:, r, t * PART:(t + 1) * PART], wo_sb[:, r, :],
                                            start=(r == 0), stop=(r == PAIRS - 2))
                last.then_inc(wo_part_done, 1)

            def wo_last(g):
                pe.wait_ge(heads_normed, last_unit + g)
                pe.wait_ge(wo_part_added, (g + 1) * NTB)
                for t in range(g * NTB, (g + 1) * NTB):
                    nc.tensor.matmul(out_half(t), attn_T[:, PAIRS - 1, t * PART:(t + 1) * PART], wo_sb[:, PAIRS - 1, :],
                                     start=True, stop=True).then_inc(wo_done, 1)

            def unit(i, u, b_, before=True, after=True):
                w, bw, iw = u + 1, 1 - b_, i + b_
                if not after:
                    pe.wait_ge(tail_loaded, 48)
                    pe.wait_ge(heads_normed, last_unit - 2)
                    pe.wait_ge(kt_copied, PIECES * UNITS)
                    pe.wait_ge(rope_terms, 2 * PIECES * UNITS)
                for j in range(ST):
                    if j < ST - 1:
                        score(u, b_, j + 1)
                    elif after:
                        score(w, bw, 0)
                    if before and j == 1:
                        sum_probs(u - 1, bw)
                    if after:
                        if 2 <= j < 2 + PIECES:
                            turn_keys(w, j - 2)
                        if j == 0:
                            project_q(iw, w, bw)
                        if j < PIECES:
                            project_kv(w, bw, j)
                    elif j % 2:
                        wo_part(j // 2)
                    if j >= 1:
                        weigh_values(u, b_, j - 1)
                    elif before:
                        weigh_values(u - 1, bw, ST - 1)

            pe.wait_ge(consts_made, 2)
            for g in range(TURNS):
                turn_rows(0, g)
            pe.wait_ge(turned_low, TURNS)
            project_q(0, 0, 0)
            project_kv(0, 0, 0)
            project_kv(0, 0, 1)
            for p in range(2, PIECES):
                turn_keys(0, p - 2)
                project_kv(0, 0, p)
            turn_keys(0, 2)
            turn_keys(0, 3)
            for g in range(TURNS):
                turn_rows(1, g)
            pe.wait_ge(turned_low, 2 * TURNS)
            score(0, 0, 0)
            unit(0, 0, 0, before=False)
            unit(0, 1, 1)
            with pe.Fori(1, PAIRS - 1) as i:
                unit(i, 2 * i, 0)
                unit(i, 2 * i + 1, 1)
            unit(PAIRS - 1, last_unit - 1, 0)
            unit(PAIRS - 1, last_unit, 1, after=False)
            weigh_values(last_unit, 1, ST - 1)
            sum_probs(last_unit, 1)

            def turn_x1(g):
                for k in range(KT):
                    for n in range(NTB):
                        t = g * NTB + n
                        pe.wait_ge(x1n_made, t + 1)
                        last = nc.tensor.transpose(psum[:, 4 + 2 * g + k, n * PART:(n + 1) * PART],
                                                   x_1n[:, t, k * PART:(k + 1) * PART], ident[:, :])
                    last.then_inc(x1_turned, 1)

            def gate_logits(g):
                pe.wait_ge(x1T_copied, KT * (g + 1))
                for n in range(NTB):
                    t = g * NTB + n
                    for k in range(KT):
                        last = nc.tensor.matmul(psum[:, 4 + 2 * g, n * E:(n + 1) * E], x_1T[:, k, t * PART:(t + 1) * PART],
                                                wg_sb[:, k, :], start=(k == 0), stop=(k == KT - 1))
                last.then_inc(logits_done, 1)

            def experts(t):
                if t % NTB == 0:
                    pe.wait_ge(x1T_low, KT * (t // NTB + 1))
                cols = slice(t * PART, (t + 1) * PART)
                for ep in range(E // 2):
                    if t > 0:
                        pe.wait_ge(ffn_added, (t - 1) * E + 2 * ep + 2)
                    else:
                        pe.wait_ge(W_low, E)
                    pair = slice(2 * ep, 2 * ep + 2)
                    terms = [(a, w_) for k in range(KT) for a, w_ in
                             ((x_1Th[:, k, cols], WT_h[:, k, pair, :]), (x_1Th[:, k, cols], WT_l[:, k, pair, :]),
                              (x_1Tl[:, k, cols], WT_h[:, k, pair, :]))]
                    for n, (a, w_) in enumerate(terms):
                        last = nc.tensor.matmul(psum[:, ep, :], a, w_.rearrange("p e f -> p (e f)"),
                                                start=(n == 0), stop=(n == len(terms) - 1))
                    last.then_inc(ffn_done, 1)

            def ranks(g):
                pe.wait_ge(consts_made, 5)
                pe.wait_ge(mask_made, g + 1)
                for n in range(NTB):
                    t = g * NTB + n
                    for t2 in range(t + 1):
                        last = nc.tensor.matmul(psum[:, 5 + 2 * g, n * E:(n + 1) * E], (upper_b if t2 == t else ones_b)[:, :],
                                                mask_b[:, t2, :], start=(t2 == 0), stop=(t2 == t))
                last.then_inc(ranks_done, 1)

            def turn_weights(g):
                pe.wait_ge(weight_made, g + 1)
                for n in range(NTB):
                    last = nc.tensor.transpose(psum[0:E, 4 + 2 * g, n * PART:(n + 1) * PART], weight[:, g * NTB + n, :],
                                               ident[:, :])
                last.then_inc(weight_turned, 1)

            def experts_bias(g):
                pe.wait_ge(weightT_copied, g + 1)
                for t in range(g * NTB, (g + 1) * NTB):
                    nc.tensor.matmul(out_half(t), weight_T[:, t * PART:(t + 1) * PART], b_sb[:, :],
                                     start=True, stop=True).then_inc(bias_done, 1)

            wo_last(0)
            for g in range(E // 2):
                turn_W(g)
            pe.wait_ge(o_copied, UNITS)
            pe.wait_ge(den_copied, UNITS)
            wo_part(NTB)
            wo_part(NTB + 1)
            turn_x1(0)
            for g in range(E // 2, E):
                turn_W(g)
            for n in range(2, NTB):
                wo_part(NTB + n)
            gate_logits(0)
            wo_last(1)
            experts(0)
            ranks(0)
            experts(1)
            turn_weights(0)
            turn_x1(1)
            experts_bias(0)
            experts(2)
            gate_logits(1)
            experts(3)
            ranks(1)
            experts(4)
            turn_weights(1)
            experts(5)
            experts_bias(1)
            for t in range(6, NT):
                experts(t)


_INS = ['x', 'ctx_1024', 'L0_xattn_cos', 'L0_xattn_sin', 'L0_xattn_ln_lat_g', 'L0_xattn_ln_lat_b', 'L0_xattn_ln_ctx_g',
        'L0_xattn_ln_ctx_b', 'L0_xattn_Wq', 'L0_xattn_Wkv', 'L0_xattn_Wo', 'L0_xattn_bo', 'L0_ffn_wg', 'L0_ffn_W', 'L0_ffn_b']
_OUTS = [((2, 512, 256), 'float32')]


def kernel(**inputs):
    import numpy as _np
    import concourse.bacc as _bacc
    from concourse import mybir as _mybir
    from concourse.bass_utils import run_bass_kernel_spmd as _run

    nc = _bacc.Bacc("TRN2", target_bir_lowering=False, num_devices=1)
    arrays, args = {}, []
    for name in _INS:
        a = _np.ascontiguousarray(inputs[name])
        arrays[f"in_{name}_dram"] = a
        args.append(nc.dram_tensor(f"in_{name}_dram", a.shape, _mybir.dt.from_np(a.dtype), kind="ExternalInput").ap())
    for i, (shape, dtype) in enumerate(_OUTS):
        dt = _mybir.dt.from_np(_np.dtype(dtype))
        args.append(nc.dram_tensor(f"out_{i}_dram", shape, dt, kind="ExternalOutput").ap())
    xattn_moe_kernel(nc, *args)
    r = _run(nc, [arrays], core_ids=[0])
    return r.results[0]["out_0_dram"]
```

```python
import concourse.bass as bass
from concourse import mybir
from concourse.alu_op_type import AluOpType as ALU
from contextlib import ExitStack
import math

FP32 = mybir.dt.float32
FP32R = mybir.dt.float32r
BF16 = mybir.dt.bfloat16
ACT = mybir.ActivationFunctionType
AX = mybir.AxisListType

PART = 128
BANK = 512
HEADS, DHEAD = 16, 64
EPS = 1e-5
CLIP = 11.0
SCALE = DHEAD ** -0.5
E_MIN, E_MAX = math.exp(-CLIP), math.exp(CLIP)


def xattn_moe_kernel(nc, x, ctx_1024, cos, sin, lat_g, lat_b, ctx_g, ctx_b, Wq, Wkv, Wo, bo, wg, W, b, out):
    BATCH, N, DIM = x.shape
    S = ctx_1024.shape[1]
    E = wg.shape[1]
    KT = DIM // PART
    NT = BATCH * N // PART
    NTB = N // PART
    ST = S // PART
    STA = BATCH * ST
    PAIRS = HEADS // 2
    PW = 2 * DHEAD
    PIECES = ST // 2
    CAP = BATCH * N // E
    assert BATCH == 2 and N == BANK and PW == PART and DIM == 256 and ST == 8

    x_v = x.rearrange("b (t p) d -> p (b t) d", p=PART)
    out_v = out.rearrange("b (t p) d -> p (b t) d", p=PART)
    ctx_v = ctx_1024.rearrange("b (t p) d -> p (b t) d", p=PART)
    cos_v = cos.rearrange("(t p) f -> p t f", p=PART)
    sin_v = sin.rearrange("(t p) f -> p t f", p=PART)
    Wq_v = Wq.rearrange("(k p) n -> p k n", p=PART)
    Wkv_v = Wkv.rearrange("(k p) (c n) -> p k c n", p=PART, c=2)
    Wo_v = Wo.rearrange("(r p) n -> p r n", p=PART)
    wg_v = wg.rearrange("(k p) e -> p k e", p=PART)
    W_v = W.rearrange("e (t p) h -> p (e t) h", p=PART)

    es = ExitStack()
    with es:
        def sb(name, shape, dt=FP32):
            return es.enter_context(nc.sbuf_tensor(name, shape, dt))

        def over(name, shape, place, dt=FP32):
            return nc.alloc_sbuf_tensor_at(name, shape, dt, offset=place)

        def sem(name):
            return es.enter_context(nc.semaphore(name))

        x_sb = sb("x_sb", [PART, NT, DIM])
        ctx_space = -(-nc.sbuf_base // 32) * 32
        ctxT_h = sb("ctxT_h", [PART, KT, STA * PART], FP32R)
        ctxT_l = sb("ctxT_l", [PART, KT, STA * PART], FP32R)
        x_space = -(-nc.sbuf_base // 32) * 32
        xT_h = sb("xT_h", [PART, KT, BATCH * N], FP32R)
        xT_l = sb("xT_l", [PART, KT, BATCH * N], FP32R)
        k_space = -(-nc.sbuf_base // 32) * 32
        k_stack = sb("k_stack", [PART, BATCH, 2, S], FP32R)
        q_high = sb("q_high", [PART, BATCH, 2, N], FP32R)
        q_low = sb("q_low", [PART, BATCH, N], FP32R)
        v_sb = sb("v_sb", [PART, BATCH, ST, PW])
        P_SLOTS = 4
        probs = sb("probs", [PART, P_SLOTS, 2, N])
        psum_acc = sb("psum_acc", [PART, BATCH, 2 * N])
        cosT = sb("cosT", [PART, ST, 2, 2, DHEAD // 2])
        sinT = sb("sinT", [PART, ST, 2, 2, DHEAD // 2])
        w_raw = sb("w_raw", [PART, KT, 3, PW])
        wkv_h = sb("wkv_h", [PART, KT, 2, PW], FP32R)
        wkv_l = sb("wkv_l", [PART, KT, 2, PW], FP32R)
        wq_h = sb("wq_h", [PART, KT, PW], FP32R)
        wq_l = sb("wq_l", [PART, KT, PW], FP32R)
        rope_a = sb("rope_a", [PART, 2, 2 * PW])
        rope_b = sb("rope_b", [PART, 2, 2 * PW])
        k_rot = sb("k_rot", [PART, 2, 2 * PW])
        kt_full = sb("kt_full", [PART, 2, BANK])
        o_raw = sb("o_raw", [PART, BATCH, N])
        den_sb = sb("den_sb", [64, BATCH, N])
        den_t = sb("den_t", [PART, BATCH, 8])
        rden_t = sb("rden_t", [PART, BATCH, 8])
        rden_b = sb("rden_b", [PART, BATCH, N])
        attn_T = sb("attn_T", [PART, PAIRS, BATCH * N])
        wo_sb = sb("wo_sb", [PART, PAIRS, DIM])
        ident = sb("ident", [PART, PART])
        ones = sb("ones", [PART, 32])
        lng = sb("lng", [PART, 4, KT])
        bo_b = sb("bo_b", [PART, DIM])
        wg_sb = sb("wg_sb", [PART, KT, E])
        b_sb = sb("b_sb", [E, DIM])
        GR = NTB + ST
        bn = sb("bn", [PART, GR, 6])
        mv = sb("mv", [PART, GR, 2])
        var = sb("var", [PART, GR])
        std = sb("std", [PART, GR])
        rs_a = sb("rs_a", [PART, GR])
        rs_b = sb("rs_b", [PART, GR])
        rstd = sb("rstd", [PART, GR])
        shift = sb("shift", [PART, ST // 2])
        ones_b = sb("ones_b", [PART, PART], BF16)
        upper_b = sb("upper_b", [PART, PART], BF16)
        rank_w = sb("rank_w", [PART, E])
        logit = sb("logit", [PART, NT, E])
        lmax = sb("lmax", [PART, NT])
        shifted = sb("shifted", [PART, NT, E])
        expd = sb("expd", [PART, NT, E])
        esum = sb("esum", [PART, NT])
        gate = sb("gate", [PART, NT])
        first = sb("first", [PART, NT, E])
        fmax = sb("fmax", [PART, NT])
        mask = sb("mask", [PART, NT, E])
        mask_b = sb("mask_b", [PART, NT, E], BF16)
        weight = sb("weight", [PART, NT, E])
        ctx_n = attn_T[:, 0:4, :].rearrange("p a (t d) -> p (a t) d", d=DIM)
        x_n = probs[:, :, :, :].rearrange("p a h (t d) -> p (a h t) d", d=DIM)[:, 0:NT, :]
        full = psum_acc[:, :, :].rearrange("p b (c n) -> p (b c) n", n=BANK)
        w_bytes, tile_bytes = 4 * KT * E * DIM, 4 * NT * DIM
        WT_h = over("WT_h", [PART, KT, E, DIM], ctx_space, FP32R)
        WT_l = over("WT_l", [PART, KT, E, DIM], ctx_space + w_bytes, FP32R)
        W_nat = over("W_nat", [PART, E * KT, DIM], x_space)
        weight_T = over("weight_T", [E, NT * PART], x_space)
        x_1 = over("x_1", [PART, NT, DIM], k_space)
        x_1n = over("x_1n", [PART, NT, DIM], k_space + tile_bytes)
        x_1T = over("x_1T", [PART, KT, NT * PART], k_space + 2 * tile_bytes)
        acc = over("acc", [PART, NT, DIM], k_space + 3 * tile_bytes)
        x_1Th = over("x_1Th", [PART, KT, NT * PART], k_space + 4 * tile_bytes, FP32R)
        x_1Tl = over("x_1Tl", [PART, KT, NT * PART], k_space + 5 * tile_bytes, FP32R)
        acc_odd = over("acc_odd", [PART, 2, DIM], k_space + 6 * tile_bytes)

        psum = es.enter_context(nc.psum_tensor("psum", [PART, 8, BANK], FP32))
        scores = [psum[:, 0:2, :], psum[:, 2:4, :]]
        PROJ = (4, 5)
        o_ps = psum[:, 6, :]
        den_ps = psum[:, 7, :]
        scratch = nc.dram_tensor("rden_scratch", [BATCH, 2 * N], FP32, kind="Internal").ap()

        x_loaded = [sem(f"x_loaded_{half}") for half in range(BATCH)]
        ctx_loaded = [sem(f"ctx_loaded_{n}") for n in range(2 * BATCH)]
        consts_loaded = sem("consts_loaded")
        sin_negated = sem("sin_negated")
        cs_loaded, tail_loaded, consts_made = sem("cs_loaded"), sem("tail_loaded"), sem("consts_made")
        dve_step = sem("dve_step")
        pool_step = sem("pool_step")
        var_ready, std_ready = sem("var_ready"), sem("std_ready")
        shift_made, act_normed = sem("shift_made"), sem("act_normed")
        ctx_normed, x_normed = sem("ctx_normed"), sem("x_normed")
        rstd_ready, turned_low_last = sem("rstd_ready"), sem("turned_low_last")
        turned_high_last = sem("turned_high_last")
        turned, turned_full, turned_high, turned_low = sem("turned"), sem("turned_full"), sem("turned_high"), sem("turned_low")
        W_turned, W_high, W_low, W_loaded = sem("W_turned"), sem("W_high"), sem("W_low"), sem("W_loaded")
        w_loaded, w_high, w_split = sem("w_loaded"), sem("w_high"), sem("w_split")
        kv_done, kt_done, q_done, q_spread = sem("kv_done"), sem("kt_done"), sem("q_done"), sem("q_spread")
        v_copied, kt_copied, q_copied, q_split = sem("v_copied"), sem("kt_copied"), sem("q_copied"), sem("q_split")
        rope_terms, k_summed, k_high, k_low = sem("rope_terms"), sem("k_summed"), sem("k_high"), sem("k_low")
        s_done, exp_done, clipped, summed = sem("s_done"), sem("exp_done"), sem("clipped"), sem("summed")
        av_done, o_copied, den_done, den_copied = sem("av_done"), sem("o_copied"), sem("den_done"), sem("den_copied")
        den_turned, rden_made, rden_stored = sem("den_turned"), sem("rden_made"), sem("rden_stored")
        rden_spread, heads_normed = sem("rden_spread"), sem("heads_normed")
        bias_added = sem("bias_added")
        wo_part_done, wo_part_added = sem("wo_part_done"), sem("wo_part_added")
        wo_done, x1_made, x1n_made = sem("wo_done"), sem("x1_made"), sem("x1n_made")
        x1_turned, x1T_copied, x1T_high, x1T_low = sem("x1_turned"), sem("x1T_copied"), sem("x1T_high"), sem("x1T_low")
        logits_done = sem("logits_done")
        shifted_made, expd_made, mask_made = sem("shifted_made"), sem("expd_made"), sem("mask_made")
        ranks_done, weight_made, weight_turned = sem("ranks_done"), sem("weight_made"), sem("weight_turned")
        weightT_copied, bias_done, tile_made = sem("weightT_copied"), sem("bias_done"), sem("tile_made")
        ffn_done, ffn_added, out_stored = sem("ffn_done"), sem("ffn_added"), sem("out_stored")

        UNITS = 2 * PAIRS
        last_unit = UNITS - 1
        TURNS = KT * (ST // 4 + 1)
        CTX_TURNS = KT * (ST // 4)
        LAST_TURNS = TURNS - CTX_TURNS
        assert CTX_TURNS == PIECES
        TURN_BANKS = (0, 1, 2, 3, 6, 7)

        def above_zero(value):
            return not isinstance(value, int) or value > 0

        def turn_group(half, g):
            t4, k = divmod(g, KT)
            if t4 < ST // 4:
                t0 = half * ST + 4 * t4
                cols = slice(t0 * PART, (t0 + 4) * PART)
                return ctx_n, t0, k, ctxT_h[:, k, cols], ctxT_l[:, k, cols], 2
            t0 = half * NTB
            cols = slice(t0 * PART, (t0 + 4) * PART)
            return x_n, t0, k, xT_h[:, k, cols], xT_l[:, k, cols], 0

        def head_rows(h):
            return slice(h * DHEAD, (h + 1) * DHEAD)

        def kv_bank(p):
            return 0 if p == 0 else 1

        block = es.enter_context(nc.Block())

        @block.sync
        def _(sp):
            for half in range(BATCH):
                ts = slice(half * NTB, (half + 1) * NTB)
                sp.dma_start(x_sb[:, ts, :], x_v[:, ts, :]).then_inc(x_loaded[half], 16)
                for h in range(2 * half, 2 * half + 2):
                    sp.dma_start(ctx_n[:, 4 * h:4 * h + 4, :], ctx_v[:, 4 * h:4 * h + 4, :]).then_inc(ctx_loaded[h], 16)

            def count(value):
                return value if isinstance(value, int) else sp.snap(sp.to_reg(value))

            sp.dma_start(w_raw[:, :, 0, :], Wq_v[:, :, 0:PW]).then_inc(w_loaded, 16)
            for c in range(2):
                sp.dma_start(w_raw[:, :, 1 + c, :], Wkv_v[:, :, c, 0:PW]).then_inc(w_loaded, 16)
            for h in range(2):
                sp.dma_start(cosT[:, :, h, 0, :], cos_v).then_inc(cs_loaded, 16)
                sp.dma_start(cosT[:, :, h, 1, :], cos_v).then_inc(cs_loaded, 16)
                sp.dma_start(sinT[:, :, h, 0, :], sin_v).then_inc(cs_loaded, 16)
                sp.dma_start(sinT[:, :, h, 1, :], sin_v).then_inc(cs_loaded, 16)
            sp.dma_start(wo_sb[:, :, :], Wo_v).then_inc(tail_loaded, 16)
            sp.dma_start(wg_sb[:, :, :], wg_v).then_inc(tail_loaded, 16)
            sp.dma_start(b_sb[:, :], b).then_inc(tail_loaded, 16)

            def sum_counts(u):
                return count(u - 1), count(u + 1), count(16 * (u + 1))

            def spread_sums(counts, b_):
                before, done, stored = counts
                sp.wait_ge(den_copied, done)
                for h in range(2):
                    sp.dma_start(den_t[64 * h:64 * h + 64, b_, :], den_sb[32 * h:32 * h + 1, b_, :]).then_inc(den_turned, 16)
                sp.wait_ge(rden_made, done)
                sp.dma_start(scratch[b_, :].rearrange("(p c) -> p c", c=8), rden_t[:, b_, :]).then_inc(rden_stored, 16)
                sp.wait_ge(rden_stored, stored)
                if above_zero(before):
                    sp.wait_ge(heads_normed, before)
                for h in range(2):
                    sp.dma_start(rden_b[64 * h:64 * h + 64, b_, :],
                                 scratch[b_:b_ + 1, h * N:(h + 1) * N].broadcast_to([64, N])).then_inc(rden_spread, 16)

            def spread_queries(done, bw):
                sp.wait_ge(q_copied, done)
                for h in range(2):
                    sp.dma_start(q_high[head_rows(1 - h), bw, h, :].bitcast(FP32),
                                 q_high[head_rows(h), bw, h, :].bitcast(FP32)).then_inc(q_spread, 16)

            def iteration(i, first=False):
                if not first:
                    sums_1 = sum_counts(2 * i - 1)
                queries_1 = count(4 * i + 4)
                sums_0 = sum_counts(2 * i)
                queries_0 = count(4 * i + 6)
                cols = bass.ds(count((i + 1) * PW), PW)
                sp.dma_start(w_raw[:, :, 0, :], Wq_v[:, :, cols]).then_inc(w_loaded, 16)
                for c in range(2):
                    sp.dma_start(w_raw[:, :, 1 + c, :], Wkv_v[:, :, c, cols]).then_inc(w_loaded, 16)
                spread_queries(queries_1, 1)
                if not first:
                    spread_sums(sums_1, 1)
                spread_queries(queries_0, 0)
                spread_sums(sums_0, 0)

            spread_queries(2, 0)
            iteration(0, first=True)
            with sp.Fori(1, PAIRS - 1) as i:
                iteration(i)
            spread_queries(2 * UNITS, 1)
            sp.dma_start(W_nat[:, :, :], W_v).then_inc(W_loaded, 16)
            spread_sums(sum_counts(last_unit - 2), 1)
            spread_sums(sum_counts(last_unit - 1), 0)
            spread_sums(sum_counts(last_unit), 1)
            parts = [(0, 4), (4, 6), (6, 7), (7, 8)]
            for first, after in parts:
                sp.wait_ge(tile_made, after)
                sp.dma_start(out_v[:, first:after, :], acc[:, first:after, :]).then_inc(out_stored, 16)
            sp.wait_ge(out_stored, 16 * len(parts))

        @block.gpsimd
        def _(pool):
            steps = [0]

            def then(ins):
                steps[0] += 1
                ins.then_inc(pool_step, 1)
                pool.wait_ge(pool_step, steps[0])

            then(nc.gpsimd.memset(ident[:, :], 0.0))
            nc.gpsimd.affine_select(out=ident[:, :], in_=ident[:, :], compare_op=ALU.not_equal, fill=1.0, base=0,
                                    pattern=[[-1, PART]], channel_multiplier=1).then_inc(consts_made, 1)
            nc.gpsimd.memset(ones[:, :], 1.0).then_inc(consts_made, 1)
            with nc.allow_non_contiguous_dma(reason="256 values each"):
                for n, v in enumerate((lat_g, lat_b, ctx_g, ctx_b)):
                    pool.dma_start(lng[:, n, :], v.rearrange("(k p) -> p k", p=PART)).then_inc(consts_loaded, 16)
            pool.dma_start(bo_b[:, :], bo.rearrange("(o n) -> o n", o=1).broadcast_to([PART, DIM])).then_inc(consts_loaded, 16)

            one = ones[:, 0:1].unsqueeze(2).unsqueeze(3)

            def split_pair(i):
                pool.wait_ge(w_loaded, 48 * (i + 1))
                if above_zero(i):
                    pool.wait_ge(q_done, 2 * i)
                nc.gpsimd.tensor_tensor(wq_h[:, :, :], w_raw[:, :, 0, :], ones[:, 0:1].unsqueeze(2).broadcast_to([PART, KT, PW]),
                                        ALU.mult).then_inc(w_high, 1)
                pool.wait_ge(w_high, 2 * i + 1)
                nc.gpsimd.tensor_tensor(wq_l[:, :, :], w_raw[:, :, 0, :], wq_h[:, :, :].bitcast(FP32),
                                        ALU.subtract).then_inc(w_split, 1)
                if above_zero(i):
                    pool.wait_ge(kv_done, 2 * PIECES * i)
                nc.gpsimd.tensor_tensor(wkv_h[:, :, :, :], w_raw[:, :, 1:3, :], one.broadcast_to([PART, KT, 2, PW]),
                                        ALU.mult).then_inc(w_high, 1)
                pool.wait_ge(w_high, 2 * (i + 1))
                nc.gpsimd.tensor_tensor(wkv_l[:, :, :, :], w_raw[:, :, 1:3, :], wkv_h[:, :, :, :].bitcast(FP32),
                                        ALU.subtract).then_inc(w_split, 1)

            def low_keys(w, bw, half):
                cols = slice(half * BANK, (half + 1) * BANK)
                for h in range(2):
                    pool.wait_ge(k_high, 4 * w + 2 * half + h + 1)
                    nc.gpsimd.tensor_tensor(k_stack[head_rows(1 - h), bw, h, cols], kt_full[head_rows(h), half, :],
                                            k_stack[head_rows(h), bw, h, cols].bitcast(FP32), ALU.subtract).then_inc(k_low, 1)
                    pool.wait_ge(k_low, 4 * w + 2 * half + h + 1)

            def iteration(i):
                split_pair(i + 1)
                pool.wait_ge(w_split, 2 * (i + 2))
                for half in range(2):
                    low_keys(2 * i + 1, 1, half)
                for half in range(2):
                    low_keys(2 * i + 2, 0, half)

            def low_turned(half, g):
                _, _, _, high, low, _ = turn_group(half, g)
                n = half * TURNS + g
                pool.wait_ge(turned_high, n + 1)
                nc.gpsimd.tensor_tensor(low, full[:, n % 4, :], high.bitcast(FP32), ALU.subtract).then_inc(turned_low, 1)

            pool.wait_ge(consts_made, 2)
            split_pair(0)
            for g in range(TURNS):
                low_turned(0, g)
            pool.wait_ge(cs_loaded, 128)
            nc.gpsimd.tensor_scalar(sinT[:, :, :, 0, :], sinT[:, :, :, 0, :], -1.0, None, ALU.mult).then_inc(sin_negated, 1)
            nc.gpsimd.memset(ones_b[:, :], 1.0).then_inc(consts_made, 1)
            then(nc.gpsimd.memset(upper_b[:, :], 0.0))
            nc.gpsimd.affine_select(out=upper_b[:, :], in_=upper_b[:, :], compare_op=ALU.is_ge, fill=1.0, base=0,
                                    pattern=[[-1, PART]], channel_multiplier=1).then_inc(consts_made, 1)
            for e in range(E):
                last = nc.gpsimd.memset(rank_w[:, e:e + 1], float(E - e))
            last.then_inc(consts_made, 1)
            for half in range(2):
                low_turned(1, 2 * half)
                low_turned(1, 2 * half + 1)
                pool.wait_ge(turned_low, TURNS + 2 * half + 2)
                low_keys(0, 0, half)
            pool.wait_ge(x_normed, 2 * BATCH)
            pool.wait_ge(consts_loaded, 80)
            for t in range(NT):
                last = nc.gpsimd.tensor_tensor(x_sb[:, t, :], x_sb[:, t, :], bo_b[:, :], ALU.add)
            last.then_inc(bias_added, 1)
            pool.wait_ge(bias_added, 1)
            iteration(0)
            with pool.Fori(1, PAIRS - 1) as i:
                iteration(i)
            for half in range(2):
                low_keys(last_unit, 1, half)

        @block.scalar
        def _(act):
            def inverse_roots(n, sl):
                act.wait_ge(var_ready, n)
                nc.scalar.activation(std[:, sl], var[:, sl], ACT.Sqrt).then_inc(std_ready, 1)

            def normalise_ctx(half):
                act.wait_ge(shift_made, half + 1)
                for n in range(ST // 2):
                    t = half * ST + n
                    nc.scalar.activation(ctx_n[:, t, :], ctx_n[:, t, :], ACT.Identity, scale=rstd[:, NTB + n:NTB + n + 1],
                                         bias=shift[:, n:n + 1]).then_inc(act_normed, 1)

            def scale_turned(half, g):
                _, _, k, high, _, c = turn_group(half, g)
                n = half * TURNS + g
                act.wait_ge(turned, n + 1)
                if n >= 4:
                    act.wait_ge(turned_low, n - 3)
                nc.scalar.activation(full[:, n % 4, :], psum[:, TURN_BANKS[g], :], ACT.Identity, scale=lng[:, c, k:k + 1],
                                     bias=lng[:, c + 1, k:k + 1]).then_inc(turned_full, 1)
                if n < BATCH * TURNS - LAST_TURNS:
                    act.wait_ge(turned_full, n + 1)
                    nc.scalar.copy(high, full[:, n % 4, :]).then_inc(turned_high, 1)

            def high_W(g):
                ep, k = divmod(g, KT)
                act.wait_ge(W_turned, g + 1)
                nc.scalar.copy(WT_h[:, k, 2 * ep:2 * ep + 2, :],
                               psum[:, g % 4, :].rearrange("p (e f) -> p e f", e=2)).then_inc(W_high, 1)

            def copy_v(w, bw, p):
                act.wait_ge(kv_done, PIECES * w + p + 1)
                nc.scalar.copy(v_sb[:, bw, 2 * p:2 * p + 2, :],
                               psum[:, PROJ[kv_bank(p)], 2 * PW:4 * PW].rearrange("p (t n) -> p t n", t=2)).then_inc(v_copied, 1)

            def copy_kt(w, half):
                act.wait_ge(kt_done, PIECES * w + 2 * half + 2)
                if above_zero(w):
                    act.wait_ge(k_low, 4 * w + 2 * half - 2)
                nc.scalar.copy(kt_full[:, half, :], psum[:, PROJ[0], :]).then_inc(kt_copied, 1)

            def high_keys(w, bw, half, h):
                act.wait_ge(kt_copied, 2 * w + half + 1)
                nc.scalar.copy(k_stack[head_rows(h), bw, h, half * BANK:(half + 1) * BANK],
                               kt_full[head_rows(h), half, :]).then_inc(k_high, 1)

            def copy_q(w, bw):
                act.wait_ge(q_done, w + 1)
                for h in range(2):
                    rows = head_rows(h)
                    nc.scalar.copy(q_high[rows, bw, h, :], psum[rows, PROJ[1], :]).then_inc(q_copied, 1)

            def copy_o(u, b_):
                act.wait_ge(av_done, ST * (u + 1))
                if above_zero(u - 1):
                    act.wait_ge(heads_normed, u - 1)
                nc.scalar.copy(o_raw[:, b_, :], o_ps).then_inc(o_copied, 1)

            def copy_den(u, b_):
                act.wait_ge(den_done, u + 1)
                if above_zero(u - 1):
                    act.wait_ge(den_turned, 32 * (u - 1))
                nc.scalar.copy(den_sb[:, b_, :], den_ps[0:64, :]).then_inc(den_copied, 1)

            def unit(u, b_, before=True, after=True):
                w, bw = u + 1, 1 - b_
                for j in range(ST):
                    c = ST * u + j
                    act.wait_ge(s_done, c + 1)
                    if above_zero(c - P_SLOTS + 1):
                        act.wait_ge(av_done, c - P_SLOTS + 1)
                        jp = (j - P_SLOTS) % ST
                        act.wait_ge(summed, (ST - 1) * (u if j >= P_SLOTS else u - 1) + max(jp, 1))
                    nc.scalar.activation(probs[:, j % P_SLOTS, :, :], scores[j % 2], ACT.Exp, scale=SCALE).then_inc(exp_done, 1)
                    if before and j == 1:
                        copy_o(u - 1, bw)
                    if before and j == 2:
                        copy_den(u - 1, bw)
                    if after:
                        if j == 0:
                            copy_q(w, bw)
                        if j == 3:
                            copy_kt(w, 0)
                        if j < PIECES:
                            copy_v(w, bw, j)
                        if j in (3, 4):
                            high_keys(w, bw, 0, j - 3)
                        if j == 5:
                            copy_kt(w, 1)
                        if j in (6, 7):
                            high_keys(w, bw, 1, j - 6)

            inverse_roots(1, slice(0, GR))
            normalise_ctx(0)
            inverse_roots(2, slice(0, NTB))
            act.wait_ge(consts_loaded, 80)
            for g in range(TURNS):
                scale_turned(0, g)
            inverse_roots(3, slice(0, GR))
            normalise_ctx(1)
            copy_q(0, 0)
            copy_v(0, 0, 0)
            copy_v(0, 0, 1)
            scale_turned(1, 0)
            copy_v(0, 0, 2)
            scale_turned(1, 1)
            inverse_roots(4, slice(0, NTB))
            copy_kt(0, 0)
            for h in range(2):
                high_keys(0, 0, 0, h)
            copy_v(0, 0, 3)
            scale_turned(1, 2)
            scale_turned(1, 3)
            for g in range(CTX_TURNS, TURNS):
                scale_turned(1, g)
            copy_kt(0, 1)
            for h in range(2):
                high_keys(0, 0, 1, h)
            unit(0, 0, before=False)
            unit(1, 1)
            with act.Fori(1, PAIRS - 1) as i:
                unit(2 * i, 0)
                unit(2 * i + 1, 1)
            unit(last_unit - 1, 0)
            unit(last_unit, 1, after=False)
            copy_o(last_unit, 1)
            copy_den(last_unit, 1)

            def roots_x1(g):
                inverse_roots(5 + g, slice(g * NTB, (g + 1) * NTB))

            def copy_x1T(g):
                cols = slice(g * N, (g + 1) * N)
                for k in range(KT):
                    act.wait_ge(x1_turned, KT * g + k + 1)
                    nc.scalar.copy(x_1T[:, k, cols], psum[:, 4 + 2 * g + k, :]).then_inc(x1T_copied, 1)
                for k in range(KT):
                    act.wait_ge(x1T_copied, KT * g + k + 1)
                    nc.scalar.copy(x_1Th[:, k, cols], x_1T[:, k, cols]).then_inc(x1T_high, 1)

            def exp_logits(g):
                ts = slice(g * NTB, (g + 1) * NTB)
                act.wait_ge(shifted_made, g + 1)
                nc.scalar.activation(expd[:, ts, :], shifted[:, ts, :], ACT.Exp).then_inc(expd_made, 1)

            def copy_weightT(g):
                act.wait_ge(weight_turned, g + 1)
                nc.scalar.copy(weight_T[:, g * N:(g + 1) * N], psum[0:E, 4 + 2 * g, :]).then_inc(weightT_copied, 1)

            for g in range(E // 2):
                high_W(g)
            roots_x1(0)
            copy_x1T(0)
            for g in range(E // 2, E):
                high_W(g)
            exp_logits(0)
            roots_x1(1)
            copy_weightT(0)
            copy_x1T(1)
            exp_logits(1)
            copy_weightT(1)

        @block.vector
        def _(dve):
            steps = [0]

            def then(ins):
                steps[0] += 1
                ins.then_inc(dve_step, 1)
                dve.wait_ge(dve_step, steps[0])

            def inverse_std(sl, ready):
                dve.wait_ge(std_ready, ready)
                then(nc.vector.reciprocal(rs_a[:, sl], std[:, sl]))
                then(nc.vector.tensor_tensor(rs_b[:, sl], rs_a[:, sl], rs_a[:, sl], ALU.mult))
                then(nc.vector.tensor_tensor(rs_b[:, sl], rs_b[:, sl], var[:, sl], ALU.mult))
                then(nc.vector.tensor_scalar(rs_b[:, sl], rs_b[:, sl], -0.5, 1.5, ALU.mult, ALU.add))
                nc.vector.tensor_tensor(rstd[:, sl], rs_a[:, sl], rs_b[:, sl], ALU.mult).then_inc(rstd_ready, 1)
                dve.wait_ge(rstd_ready, ready)

            def stats(tiles, at):
                for t in range(tiles.shape[1]):
                    last = nc.vector.bn_stats(bn[:, at + t, :], tiles[:, t, :])
                then(last)
                for t in range(tiles.shape[1]):
                    last = nc.vector.bn_aggr(mv[:, at + t, :], bn[:, at + t, :])
                then(last)

            def add_eps(sl):
                nc.vector.tensor_scalar(var[:, sl], mv[:, sl, 1], EPS, None, ALU.add).then_inc(var_ready, 1)

            def normalise(dst, src, t, at):
                return nc.vector.tensor_scalar(dst[:, t, :], src[:, t, :], mv[:, at + t, 0:1], rstd[:, at + t:at + t + 1],
                                               ALU.subtract, ALU.mult)

            def x_stats(half):
                dve.wait_ge(x_loaded[half], 16)
                stats(x_sb[:, half * NTB:(half + 1) * NTB, :], 0)

            def ctx_stats(half):
                for n in range(2):
                    dve.wait_ge(ctx_loaded[2 * half + n], 16)
                    t0 = half * ST + n * ST // 2
                    stats(ctx_n[:, t0:t0 + ST // 2, :], NTB + n * ST // 2)
                add_eps(slice(0, GR))

            def normalise_rows(half):
                x0, c0 = half * NTB, half * ST
                if half:
                    dve.wait_ge(act_normed, ST // 2)
                inverse_std(slice(0, GR), 2 * half + 1)
                nc.vector.scalar_tensor_tensor(out=shift[:, :], in0=mv[:, NTB:NTB + ST // 2, 0], scalar=-1.0,
                                               in1=rstd[:, NTB:NTB + ST // 2], op0=ALU.mult, op1=ALU.mult).then_inc(shift_made, 1)
                for t in range(NTB):
                    last = normalise(x_n, x_sb, x0 + t, -x0)
                then(last)
                for t in range(ST // 2, ST):
                    normalise(ctx_n, ctx_n, c0 + t, NTB - c0).then_inc(ctx_normed, 1)

            def stats_again(half):
                x0 = half * NTB
                stats(x_n[:, x0:x0 + NTB, :], 0)
                add_eps(slice(0, NTB))

            def normalise_x_again(half):
                x0 = half * NTB
                inverse_std(slice(0, NTB), 2 * half + 2)
                for t in range(NTB):
                    last = normalise(x_n, x_n, x0 + t, -x0)
                last.then_inc(x_normed, 2)

            def split_turned(half, g):
                _, _, _, high, low, _ = turn_group(half, g)
                n = half * TURNS + g
                dve.wait_ge(turned_full, n + 1)
                nc.vector.tensor_copy(high, full[:, n % 4, :]).then_inc(turned_high_last, 1)
                dve.wait_ge(turned_high_last, g - CTX_TURNS + 1)
                nc.vector.tensor_tensor(low, full[:, n % 4, :], high.bitcast(FP32), ALU.subtract).then_inc(turned_low_last, 1)

            def rope(w, p):
                t = PIECES * w + p
                src = psum[:, PROJ[kv_bank(p)], 0:2 * PW].rearrange("p (a f c) -> p a f c", f=2, c=DHEAD // 2)
                cosv = cosT[:, 2 * p:2 * p + 2, :, :, :].rearrange("p t h f c -> p (t h) f c")
                sinv = sinT[:, 2 * p:2 * p + 2, :, :, :].rearrange("p t h f c -> p (t h) f c")
                a, bb, kr = rope_a[:, p % 2, :], rope_b[:, p % 2, :], k_rot[:, p % 2, :]
                a4 = a.rearrange("p (a f c) -> p a f c", f=2, c=DHEAD // 2)
                b4 = bb.rearrange("p (a f c) -> p a f c", f=2, c=DHEAD // 2)
                dve.wait_ge(v_copied, t + 1)
                nc.vector.tensor_tensor(a4, src, cosv, ALU.mult).then_inc(rope_terms, 1)
                nc.vector.tensor_tensor(b4, src[:, :, ::-1, :], sinv, ALU.mult).then_inc(rope_terms, 1)
                dve.wait_ge(rope_terms, 2 * (t + 1))
                if above_zero(t - 1):
                    dve.wait_ge(kt_done, t - 1)
                nc.vector.tensor_tensor(kr, a, bb, ALU.add).then_inc(k_summed, 1)

            def split_q(w, bw):
                dve.wait_ge(q_copied, 2 * (w + 1))
                for h in range(2):
                    rows = head_rows(h)
                    nc.vector.tensor_tensor(q_low[rows, bw, :], psum[rows, PROJ[1], :], q_high[rows, bw, h, :].bitcast(FP32),
                                            ALU.subtract).then_inc(q_split, 1)

            def invert_sums(u, b_):
                dve.wait_ge(den_turned, 32 * (u + 1))
                if above_zero(u - 1):
                    dve.wait_ge(rden_stored, 16 * (u - 1))
                nc.vector.reciprocal(rden_t[:, b_, :], den_t[:, b_, :]).then_inc(rden_made, 1)

            def norm_heads(i, u, b_):
                dve.wait_ge(rden_spread, 32 * (u + 1))
                dve.wait_ge(o_copied, u + 1)
                dst = attn_T[:, bass.ds(i, 1), b_ * N:(b_ + 1) * N].rearrange("p o n -> p (o n)")
                nc.vector.tensor_tensor(dst, o_raw[:, b_, :], rden_b[:, b_, :], ALU.mult).then_inc(heads_normed, 1)

            def add_part(t):
                dve.wait_ge(wo_part_done, t - t % 2 + 2)
                nc.vector.tensor_tensor(x_sb[:, t, :], psum[:, 4 + t // 2, (t % 2) * DIM:(t % 2 + 1) * DIM],
                                        x_sb[:, t, :], ALU.add).then_inc(wo_part_added, 1)

            def unit(i, u, b_, before=1, after=True):
                w, bw = u + 1, 1 - b_
                for j in range(ST):
                    c = ST * u + j
                    chunk = probs[:, j % P_SLOTS, :, :].rearrange("p h n -> p (h n)")
                    dve.wait_ge(exp_done, c + 1)
                    nc.vector.tensor_scalar(chunk, chunk, E_MIN, E_MAX, ALU.max, ALU.min).then_inc(clipped, 1)
                    if j >= 1:
                        dve.wait_ge(clipped, c + 1)
                        if j == 1 and before >= 2:
                            dve.wait_ge(den_done, u - 1)
                        if j >= 2:
                            dve.wait_ge(summed, (ST - 1) * u + j - 1)
                        prev = probs[:, 0, :, :].rearrange("p h n -> p (h n)") if j == 1 else psum_acc[:, b_, :]
                        nc.vector.tensor_tensor(psum_acc[:, b_, :], prev, chunk, ALU.add).then_inc(summed, 1)
                    if j == 1 and before >= 2:
                        norm_heads(i - 1, u - 2, b_)
                    if not after and 5 <= j < 7:
                        add_part(j - 5)
                    if after and j == 0:
                        split_q(w, bw)
                    if after and j < PIECES:
                        rope(w, j)
                    if j == 5 and before >= 1:
                        invert_sums(u - 1, bw)

            x_stats(0)
            ctx_stats(0)
            normalise_rows(0)
            stats_again(0)
            normalise_x_again(0)
            x_stats(1)
            ctx_stats(1)
            normalise_rows(1)
            dve.wait_ge(cs_loaded, 128)
            dve.wait_ge(sin_negated, 1)
            split_q(0, 0)
            rope(0, 0)
            rope(0, 1)
            stats_again(1)
            rope(0, 2)
            normalise_x_again(1)
            rope(0, 3)
            for g in range(CTX_TURNS, TURNS):
                split_turned(1, g)
            unit(0, 0, 0, before=0)
            unit(0, 1, 1, before=1)
            with dve.Fori(1, PAIRS - 1) as i:
                unit(i, 2 * i, 0, before=2)
                unit(i, 2 * i + 1, 1, before=2)
            unit(PAIRS - 1, last_unit - 1, 0, before=2)
            unit(PAIRS - 1, last_unit, 1, before=2, after=False)
            norm_heads(PAIRS - 1, last_unit - 1, 0)
            add_part(2)
            add_part(3)

            def slices(g):
                return slice(g * NTB, (g + 1) * NTB), range(g * NTB, (g + 1) * NTB)

            def x1_stats(g):
                ts, tiles = slices(g)
                for t in tiles:
                    dve.wait_ge(wo_done, t - t % 2 + 2)
                    nc.vector.tensor_tensor(x_1[:, t, :], psum[:, 4 + t // 2, (t % 2) * DIM:(t % 2 + 1) * DIM],
                                            x_sb[:, t, :], ALU.add).then_inc(x1_made, 1)
                dve.wait_ge(x1_made, (g + 1) * NTB)
                stats(x_1[:, ts, :], g * NTB)
                add_eps(ts)

            def x1_normalise(g):
                ts, tiles = slices(g)
                inverse_std(ts, 5 + g)
                for t in tiles:
                    normalise(x_1n, x_1, t, 0).then_inc(x1n_made, 1)

            def low_W(g):
                ep, k = divmod(g, KT)
                dve.wait_ge(W_high, g + 1)
                nc.vector.tensor_tensor(WT_l[:, k, 2 * ep:2 * ep + 2, :], psum[:, g % 4, :].rearrange("p (e f) -> p e f", e=2),
                                        WT_h[:, k, 2 * ep:2 * ep + 2, :].bitcast(FP32), ALU.subtract).then_inc(W_low, 1)

            def low_x1T(g):
                cols = slice(g * N, (g + 1) * N)
                for k in range(KT):
                    dve.wait_ge(x1T_high, KT * g + k + 1)
                    nc.vector.tensor_tensor(x_1Tl[:, k, cols], x_1T[:, k, cols], x_1Th[:, k, cols].bitcast(FP32),
                                            ALU.subtract).then_inc(x1T_low, 1)

            def choose(g):
                ts, _ = slices(g)
                dve.wait_ge(logits_done, g + 1)
                then(nc.vector.tensor_copy(logit[:, ts, :], psum[:, 4 + 2 * g, 0:NTB * E].rearrange("p (t e) -> p t e", e=E)))
                then(nc.vector.reduce_max(lmax[:, ts], logit[:, ts, :], AX.X))
                nc.vector.tensor_tensor(shifted[:, ts, :], logit[:, ts, :], lmax[:, ts].unsqueeze(2).broadcast_to([PART, NTB, E]),
                                        ALU.subtract).then_inc(shifted_made, 1)
                dve.wait_ge(shifted_made, g + 1)
                dve.wait_ge(consts_made, 5)
                then(nc.vector.scalar_tensor_tensor(out=first[:, ts, :], in0=shifted[:, ts, :], scalar=0.0,
                                                    in1=rank_w[:, :].unsqueeze(1).broadcast_to([PART, NTB, E]),
                                                    op0=ALU.is_equal, op1=ALU.mult))
                then(nc.vector.reduce_max(fmax[:, ts], first[:, ts, :], AX.X))
                then(nc.vector.tensor_tensor(mask[:, ts, :], first[:, ts, :], fmax[:, ts].unsqueeze(2).broadcast_to([PART, NTB, E]),
                                             ALU.is_equal))
                nc.vector.tensor_copy(mask_b[:, ts, :], mask[:, ts, :]).then_inc(mask_made, 1)
                dve.wait_ge(expd_made, g + 1)
                then(nc.vector.reduce_sum(esum[:, ts], expd[:, ts, :], AX.X))
                then(nc.vector.reciprocal(gate[:, ts], esum[:, ts]))

            def weigh_tokens(g):
                ts, _ = slices(g)
                dve.wait_ge(ranks_done, g + 1)
                then(nc.vector.scalar_tensor_tensor(out=weight[:, ts, :],
                                                    in0=psum[:, 5 + 2 * g, 0:NTB * E].rearrange("p (t e) -> p t e", e=E),
                                                    scalar=float(CAP), in1=mask[:, ts, :], op0=ALU.is_lt, op1=ALU.mult))
                nc.vector.tensor_tensor(weight[:, ts, :], weight[:, ts, :], gate[:, ts].unsqueeze(2).broadcast_to([PART, NTB, E]),
                                        ALU.mult).then_inc(weight_made, 1)
                dve.wait_ge(weight_made, g + 1)

            def add_experts(t, with_bias=False):
                if with_bias:
                    then(nc.vector.tensor_tensor(x_1[:, t, :], bias_of(t), x_1[:, t, :], ALU.add))
                odd = acc_odd[:, t % 2, :]
                for e in range(E):
                    out_e = psum[:, e // 2, (e % 2) * DIM:(e % 2 + 1) * DIM]
                    w_e = weight[:, t, e:e + 1]
                    dve.wait_ge(ffn_done, (t * E + e) // 2 + 1)
                    if e == 1:
                        nc.vector.tensor_scalar(odd, out_e, w_e, None, ALU.mult).then_inc(ffn_added, 1)
                        continue
                    if e >= 2:
                        dve.wait_ge(ffn_added, t * E + e - 1)
                    sum_ = odd if e % 2 else acc[:, t, :]
                    nc.vector.scalar_tensor_tensor(out=sum_, in0=out_e, scalar=w_e, in1=sum_ if e else x_1[:, t, :],
                                                   op0=ALU.mult, op1=ALU.add).then_inc(ffn_added, 1)
                dve.wait_ge(ffn_added, (t + 1) * E)
                both = nc.vector.tensor_tensor(acc[:, t, :], acc[:, t, :], odd, ALU.add)
                if with_bias:
                    both.then_inc(tile_made, 1)
                else:
                    then(both)

            def bias_of(t):
                dve.wait_ge(bias_done, t - t % 2 + 2)
                return psum[:, 4 + t // 2, (t % 2) * DIM:(t % 2 + 1) * DIM]

            def add_bias(t):
                nc.vector.tensor_tensor(acc[:, t, :], bias_of(t), acc[:, t, :], ALU.add).then_inc(tile_made, 1)

            dve.wait_ge(bias_added, 1)
            x1_stats(0)
            invert_sums(last_unit, 1)
            x1_normalise(0)
            for g in range(E // 2):
                low_W(g)
            for n in range(2):
                add_part(NTB + n)
            for g in range(E // 2, E):
                low_W(g)
            norm_heads(PAIRS - 1, last_unit, 1)
            low_x1T(0)
            for n in range(2, NTB):
                add_part(NTB + n)
            choose(0)
            weigh_tokens(0)
            x1_stats(1)
            x1_normalise(1)
            add_experts(0)
            add_experts(1)
            choose(1)
            add_experts(2)
            weigh_tokens(1)
            low_x1T(1)
            add_experts(3)
            for t in range(NTB):
                add_bias(t)
            add_experts(NTB)
            add_bias(NTB)
            for t in range(NTB + 1, NT):
                add_experts(t, with_bias=True)

        @block.tensor
        def _(pe):
            def turn_rows(half, g):
                src, t0, k, _, _, _ = turn_group(half, g)
                if src is ctx_n and t0 % ST:
                    pe.wait_ge(ctx_normed, (half + 1) * ST // 2)
                elif src is ctx_n:
                    pe.wait_ge(act_normed, (half + 1) * ST // 2)
                else:
                    pe.wait_ge(x_normed, 2 * (half + 1))
                if half:
                    pe.wait_ge(turned_full, g + 1)
                for n in range(4):
                    last = nc.tensor.transpose(psum[:, TURN_BANKS[g], n * PART:(n + 1) * PART],
                                               src[:, t0 + n, k * PART:(k + 1) * PART], ident[:, :])
                last.then_inc(turned, 1)

            def project_kv(w, bw, p):
                if p == 0:
                    if above_zero(w):
                        pe.wait_ge(kt_copied, 2 * w)
                elif p == 1:
                    pe.wait_ge(q_split, 2 * (w + 1))
                else:
                    pe.wait_ge(rope_terms, 2 * (PIECES * w + p))
                bank = psum[:, PROJ[kv_bank(p)], :].rearrange("p (c t n) -> p c t n", c=2, t=2)
                for t in range(2):
                    cols = slice((bw * ST + 2 * p + t) * PART, (bw * ST + 2 * p + t + 1) * PART)
                    terms = [(a, w_) for k in range(KT) for a, w_ in
                             ((ctxT_h[:, k, cols], wkv_h[:, k, :, :]), (ctxT_h[:, k, cols], wkv_l[:, k, :, :]),
                              (ctxT_l[:, k, cols], wkv_h[:, k, :, :]))]
                    for n, (a, w_) in enumerate(terms):
                        last = nc.tensor.matmul(bank[:, :, t, :], a, w_, start=(n == 0), stop=(n == len(terms) - 1))
                last.then_inc(kv_done, 1)

            def turn_keys(w, p):
                pe.wait_ge(k_summed, PIECES * w + p + 1)
                if p == 2:
                    pe.wait_ge(kt_copied, 2 * w + 1)
                for t in range(2):
                    cols = slice((2 * (p % 2) + t) * PART, (2 * (p % 2) + t + 1) * PART)
                    last = nc.tensor.transpose(psum[:, PROJ[0], cols], k_rot[:, p % 2, t * PW:(t + 1) * PW], ident[:, :])
                last.then_inc(kt_done, 1)

            def project_q(i, w, bw):
                pe.wait_ge(w_split, 2 * (i + 1))
                if above_zero(w):
                    pe.wait_ge(rope_terms, 2 * PIECES * w)
                cols = slice(bw * N, (bw + 1) * N)
                terms = [(w_, a) for k in range(KT) for w_, a in
                         ((wq_h[:, k, :], xT_h[:, k, cols]), (wq_h[:, k, :], xT_l[:, k, cols]),
                          (wq_l[:, k, :], xT_h[:, k, cols]))]
                for n, (w_, a) in enumerate(terms):
                    last = nc.tensor.matmul(psum[:, PROJ[1], :], w_, a, start=(n == 0), stop=(n == len(terms) - 1))
                last.then_inc(q_done, 1)

            def score(u, b_, j):
                c = ST * u + j
                if j == 0:
                    pe.wait_ge(k_low, 4 * u + 2)
                    pe.wait_ge(q_split, 2 * (u + 1))
                    pe.wait_ge(q_spread, 32 * (u + 1))
                if j == ST // 2:
                    pe.wait_ge(k_low, 4 * u + 4)
                if above_zero(c - 1):
                    pe.wait_ge(exp_done, c - 1)
                keys = k_stack[:, b_, :, j * PART:(j + 1) * PART]
                for h in range(2):
                    nc.tensor.matmul(scores[j % 2][:, h, :], keys[:, h, :], q_high[:, b_, h, :], start=True, stop=False)
                for h in range(2):
                    last = nc.tensor.matmul(scores[j % 2][:, h, :], keys[head_rows(h), h, :], q_low[head_rows(h), b_, :],
                                            start=False, stop=True)
                last.then_inc(s_done, 1)

            def weigh_values(u, b_, j):
                if j == 0:
                    pe.wait_ge(v_copied, PIECES * (u + 1))
                    if above_zero(u):
                        pe.wait_ge(o_copied, u)
                pe.wait_ge(clipped, ST * u + j + 1)
                for h in range(2):
                    last = nc.tensor.matmul(o_ps[64 * h:64 * h + 64, :], v_sb[:, b_, j, h * DHEAD:(h + 1) * DHEAD],
                                            probs[:, j % P_SLOTS, h, :], start=(j == 0), stop=(j == ST - 1))
                last.then_inc(av_done, 1)

            def sum_probs(u, b_):
                pe.wait_ge(summed, (ST - 1) * (u + 1))
                if above_zero(u):
                    pe.wait_ge(den_copied, u)
                for h in range(2):
                    last = nc.tensor.matmul(den_ps[32 * h:32 * h + 32, :], ones[:, :], psum_acc[:, b_, h * N:(h + 1) * N],
                                            start=True, stop=True)
                last.then_inc(den_done, 1)

            def turn_W(g):
                ep, k = divmod(g, KT)
                if g == 0:
                    pe.wait_ge(exp_done, ST * UNITS)
                    pe.wait_ge(W_loaded, 16)
                if g >= 4:
                    pe.wait_ge(W_low, g - 3)
                for n in range(4):
                    last = nc.tensor.transpose(psum[:, g % 4, n * PART:(n + 1) * PART],
                                               W_nat[:, 4 * ep + n, k * PART:(k + 1) * PART], ident[:, :])
                last.then_inc(W_turned, 1)

            def out_half(t):
                return psum[:, 4 + t // 2, (t % 2) * DIM:(t % 2 + 1) * DIM]

            def wo_part(t, pairs=range(PAIRS - 1)):
                for r in pairs:
                    last = nc.tensor.matmul(out_half(t), attn_T[:, r, t * PART:(t + 1) * PART], wo_sb[:, r, :],
                                            start=(r == 0), stop=(r == PAIRS - 2))
                if r == PAIRS - 2:
                    last.then_inc(wo_part_done, 1)

            def wo_last(g):
                pe.wait_ge(heads_normed, last_unit + g)
                pe.wait_ge(wo_part_added, (g + 1) * NTB)
                for t in range(g * NTB, (g + 1) * NTB):
                    nc.tensor.matmul(out_half(t), attn_T[:, PAIRS - 1, t * PART:(t + 1) * PART], wo_sb[:, PAIRS - 1, :],
                                     start=True, stop=True).then_inc(wo_done, 1)

            def unit(i, u, b_, before=True, after=True):
                w, bw, iw = u + 1, 1 - b_, i + b_
                if not after:
                    pe.wait_ge(tail_loaded, 48)
                    pe.wait_ge(heads_normed, last_unit - 2)
                    pe.wait_ge(kt_copied, 2 * UNITS)
                    pe.wait_ge(rope_terms, 2 * PIECES * UNITS)
                for j in range(ST):
                    if j < ST - 1:
                        score(u, b_, j + 1)
                    elif after:
                        score(w, bw, 0)
                    if after:
                        if j == 0 and not before:
                            pe.wait_ge(turned_low, TURNS + CTX_TURNS)
                            pe.wait_ge(turned_low_last, LAST_TURNS)
                        if j == 0:
                            project_q(iw, w, bw)
                        if j < PIECES:
                            project_kv(w, bw, j)
                    elif j % 2:
                        wo_part(j // 2, range(PAIRS // 2, PAIRS - 1))
                    else:
                        wo_part(j // 2, range(PAIRS // 2))
                    if j >= 1:
                        weigh_values(u, b_, j - 1)
                    elif before:
                        weigh_values(u - 1, bw, ST - 1)
                    if before and j == 1:
                        sum_probs(u - 1, bw)
                    if after and 1 <= j < 1 + PIECES:
                        turn_keys(w, j - 1)

            pe.wait_ge(consts_made, 2)
            for g in range(TURNS):
                turn_rows(0, g)
            pe.wait_ge(turned_low, TURNS)
            project_q(0, 0, 0)
            project_kv(0, 0, 0)
            project_kv(0, 0, 1)
            for p in range(2, PIECES):
                turn_rows(1, p - 2)
                turn_keys(0, p - 2)
                project_kv(0, 0, p)
            turn_rows(1, 2)
            turn_keys(0, 2)
            turn_rows(1, 3)
            for g in range(CTX_TURNS, TURNS):
                turn_rows(1, g)
            turn_keys(0, 3)
            pe.wait_ge(turned_full, TURNS + 4)
            score(0, 0, 0)
            unit(0, 0, 0, before=False)
            unit(0, 1, 1)
            with pe.Fori(1, PAIRS - 1) as i:
                unit(i, 2 * i, 0)
                unit(i, 2 * i + 1, 1)
            unit(PAIRS - 1, last_unit - 1, 0)
            unit(PAIRS - 1, last_unit, 1, after=False)
            weigh_values(last_unit, 1, ST - 1)
            sum_probs(last_unit, 1)

            def turn_x1(g):
                for k in range(KT):
                    for n in range(NTB):
                        t = g * NTB + n
                        pe.wait_ge(x1n_made, t + 1)
                        last = nc.tensor.transpose(psum[:, 4 + 2 * g + k, n * PART:(n + 1) * PART],
                                                   x_1n[:, t, k * PART:(k + 1) * PART], ident[:, :])
                    last.then_inc(x1_turned, 1)

            def gate_logits(g):
                pe.wait_ge(x1T_copied, KT * (g + 1))
                for n in range(NTB):
                    t = g * NTB + n
                    for k in range(KT):
                        last = nc.tensor.matmul(psum[:, 4 + 2 * g, n * E:(n + 1) * E], x_1T[:, k, t * PART:(t + 1) * PART],
                                                wg_sb[:, k, :], start=(k == 0), stop=(k == KT - 1))
                last.then_inc(logits_done, 1)

            def experts(t, pairs=range(E // 2)):
                if t % NTB == 0:
                    pe.wait_ge(x1T_low, KT * (t // NTB + 1))
                cols = slice(t * PART, (t + 1) * PART)
                for ep in pairs:
                    if t > 0:
                        pe.wait_ge(ffn_added, (t - 1) * E + 2 * ep + 2)
                    else:
                        pe.wait_ge(W_low, E)
                    pair = slice(2 * ep, 2 * ep + 2)
                    terms = [(a, w_) for k in range(KT) for a, w_ in
                             ((x_1Th[:, k, cols], WT_h[:, k, pair, :]), (x_1Th[:, k, cols], WT_l[:, k, pair, :]),
                              (x_1Tl[:, k, cols], WT_h[:, k, pair, :]))]
                    for n, (a, w_) in enumerate(terms):
                        last = nc.tensor.matmul(psum[:, ep, :], a, w_.rearrange("p e f -> p (e f)"),
                                                start=(n == 0), stop=(n == len(terms) - 1))
                    last.then_inc(ffn_done, 1)

            def ranks(g):
                pe.wait_ge(consts_made, 5)
                pe.wait_ge(mask_made, g + 1)
                for n in range(NTB):
                    t = g * NTB + n
                    for t2 in range(t + 1):
                        last = nc.tensor.matmul(psum[:, 5 + 2 * g, n * E:(n + 1) * E], (upper_b if t2 == t else ones_b)[:, :],
                                                mask_b[:, t2, :], start=(t2 == 0), stop=(t2 == t))
                last.then_inc(ranks_done, 1)

            def turn_weights(g):
                pe.wait_ge(weight_made, g + 1)
                for n in range(NTB):
                    last = nc.tensor.transpose(psum[0:E, 4 + 2 * g, n * PART:(n + 1) * PART], weight[:, g * NTB + n, :],
                                               ident[:, :])
                last.then_inc(weight_turned, 1)

            def experts_bias(g):
                pe.wait_ge(weightT_copied, g + 1)
                for t in range(g * NTB, (g + 1) * NTB):
                    nc.tensor.matmul(out_half(t), weight_T[:, t * PART:(t + 1) * PART], b_sb[:, :],
                                     start=True, stop=True).then_inc(bias_done, 1)

            wo_last(0)
            for g in range(E // 2):
                turn_W(g)
            pe.wait_ge(o_copied, UNITS)
            pe.wait_ge(den_copied, UNITS)
            wo_part(NTB)
            wo_part(NTB + 1)
            turn_x1(0)
            for g in range(E // 2, E):
                turn_W(g)
            for n in range(2, NTB):
                wo_part(NTB + n)
            gate_logits(0)
            wo_last(1)
            ranks(0)
            experts(0, range(E // 4))
            turn_weights(0)
            experts(0, range(E // 4, E // 2))
            experts_bias(0)
            turn_x1(1)
            experts(1)
            gate_logits(1)
            experts(2)
            ranks(1)
            experts(3)
            turn_weights(1)
            experts(4)
            experts_bias(1)
            for t in range(5, NT):
                experts(t)


_INS = ['x', 'ctx_1024', 'L0_xattn_cos', 'L0_xattn_sin', 'L0_xattn_ln_lat_g', 'L0_xattn_ln_lat_b', 'L0_xattn_ln_ctx_g',
        'L0_xattn_ln_ctx_b', 'L0_xattn_Wq', 'L0_xattn_Wkv', 'L0_xattn_Wo', 'L0_xattn_bo', 'L0_ffn_wg', 'L0_ffn_W', 'L0_ffn_b']
_OUTS = [((2, 512, 256), 'float32')]


def kernel(**inputs):
    import numpy as _np
    import concourse.bacc as _bacc
    from concourse import mybir as _mybir
    from concourse.bass_utils import run_bass_kernel_spmd as _run

    nc = _bacc.Bacc("TRN2", target_bir_lowering=False, num_devices=1)
    arrays, args = {}, []
    for name in _INS:
        a = _np.ascontiguousarray(inputs[name])
        arrays[f"in_{name}_dram"] = a
        args.append(nc.dram_tensor(f"in_{name}_dram", a.shape, _mybir.dt.from_np(a.dtype), kind="ExternalInput").ap())
    for i, (shape, dtype) in enumerate(_OUTS):
        dt = _mybir.dt.from_np(_np.dtype(dtype))
        args.append(nc.dram_tensor(f"out_{i}_dram", shape, dt, kind="ExternalOutput").ap())
    xattn_moe_kernel(nc, *args)
    r = _run(nc, [arrays], core_ids=[0])
    return r.results[0]["out_0_dram"]
```
